# Optimizing a Trainium2 kernel written in Bass

```python
import numpy as np
import jax
import jax.numpy as jnp

def _softmax(x, axis=-1):
    return jax.nn.softmax(x, axis=axis)

def _gelu(x):
    return jax.nn.gelu(x, approximate=True)

def _silu(x):
    return jax.nn.silu(x)

def _sigmoid(x):
    return jax.nn.sigmoid(x)

def _layernorm(x, axis=-1, eps=1e-05):
    m = jnp.mean(x, axis=axis, keepdims=True)
    v = jnp.var(x, axis=axis, keepdims=True)
    return (x - m) / jnp.sqrt(v + eps)

def _scatter_add(tgt, idx, src, axis=0):
    return tgt.at[idx].add(src)

def _segment_sum(src, seg, n):
    return jax.ops.segment_sum(src, seg, n)
kernel_name = 'mk_gnn_preln_d1_gnn_r8_18fdc4'

def setup_inputs(seed: int=0):
    np.random.seed(seed)
    _w = jnp.asarray

    def _rec_inputs():
        import jax
        import jax.numpy as jnp
        _gk = jax.random.key(seed)
        x = -8.776e-05 + 1 * jax.random.normal(jax.random.fold_in(_gk, 1), (12500, 128), jnp.float32)
        src = jax.random.randint(jax.random.fold_in(_gk, 2), (400000,), 0, 12500, jnp.int32)
        dst = jnp.minimum((12500 * jax.random.uniform(jax.random.fold_in(_gk, 3), (400000,)) ** 2.0).astype(jnp.int32), 99999)
        _o = jnp.argsort(dst, stable=True)
        src = src[_o]
        dst = dst[_o]
        edge_attr_64 = 0.000167468 + 1.0002 * jax.random.normal(jax.random.fold_in(_gk, 11), (400000, 64), jnp.float32)
        return (x, src, dst, edge_attr_64)
    x, src, dst, edge_attr_64 = _rec_inputs()

    def _L0_gnn_setup():
        import jax, jax.numpy as jnp
        import numpy as np
        N_NODES = 5000
        N_EDGES = 80000
        ATOM_DIM = 128
        BOND_DIM = 64
        HIDDEN = 128
        key = jax.random.key(seed)
        ks = jax.random.split(key, 11)
        x = jax.random.normal(ks[0], (N_NODES, ATOM_DIM), dtype=jnp.float32)
        edge_index = jax.random.randint(ks[1], (2, N_EDGES), 0, N_NODES, dtype=jnp.int64)
        edge_attr = jax.random.normal(ks[2], (N_EDGES, BOND_DIM), dtype=jnp.float32)
        s1 = 1.0 / np.sqrt(ATOM_DIM + BOND_DIM)
        s2 = 1.0 / np.sqrt(HIDDEN)
        s3 = 1.0 / np.sqrt(ATOM_DIM + HIDDEN)
        msg_w1 = jax.random.uniform(ks[3], (ATOM_DIM + BOND_DIM, HIDDEN), minval=-s1, maxval=s1, dtype=jnp.float32)
        msg_b1 = jax.random.uniform(ks[4], (HIDDEN,), minval=-s1, maxval=s1, dtype=jnp.float32)
        msg_w2 = jax.random.uniform(ks[5], (HIDDEN, HIDDEN), minval=-s2, maxval=s2, dtype=jnp.float32)
        msg_b2 = jax.random.uniform(ks[6], (HIDDEN,), minval=-s2, maxval=s2, dtype=jnp.float32)
        upd_w1 = jax.random.uniform(ks[7], (ATOM_DIM + HIDDEN, HIDDEN), minval=-s3, maxval=s3, dtype=jnp.float32)
        upd_b1 = jax.random.uniform(ks[8], (HIDDEN,), minval=-s3, maxval=s3, dtype=jnp.float32)
        upd_w2 = jax.random.uniform(ks[9], (HIDDEN, HIDDEN), minval=-s2, maxval=s2, dtype=jnp.float32)
        upd_b2 = jax.random.uniform(ks[10], (HIDDEN,), minval=-s2, maxval=s2, dtype=jnp.float32)
        return {'x': x, 'edge_index': edge_index, 'edge_attr': edge_attr, 'msg_w1': msg_w1, 'msg_b1': msg_b1, 'msg_w2': msg_w2, 'msg_b2': msg_b2, 'upd_w1': upd_w1, 'upd_b1': upd_b1, 'upd_w2': upd_w2, 'upd_b2': upd_b2}
    _L0_gnn_all = _L0_gnn_setup()
    _L0_gnn_in = {k: v for k, v in _L0_gnn_all.items() if k in ('msg_w1', 'msg_b1', 'msg_w2', 'msg_b2', 'upd_w1', 'upd_b1', 'upd_w2', 'upd_b2')}
    del _L0_gnn_all
    return {'x': x, 'src': src, 'dst': dst, 'edge_attr_64': edge_attr_64, 'L0_gnn_msg_w1': _L0_gnn_in['msg_w1'], 'L0_gnn_msg_b1': _L0_gnn_in['msg_b1'], 'L0_gnn_msg_w2': _L0_gnn_in['msg_w2'], 'L0_gnn_msg_b2': _L0_gnn_in['msg_b2'], 'L0_gnn_upd_w1': _L0_gnn_in['upd_w1'], 'L0_gnn_upd_b1': _L0_gnn_in['upd_b1'], 'L0_gnn_upd_w2': _L0_gnn_in['upd_w2'], 'L0_gnn_upd_b2': _L0_gnn_in['upd_b2']}

def reference(x, src, dst, edge_attr_64, L0_gnn_msg_w1, L0_gnn_msg_b1, L0_gnn_msg_w2, L0_gnn_msg_b2, L0_gnn_upd_w1, L0_gnn_upd_b1, L0_gnn_upd_w2, L0_gnn_upd_b2):
    import jax
    import jax.numpy as jnp

    def _L0_gnn_ref(x, edge_index, edge_attr, msg_w1, msg_b1, msg_w2, msg_b2, upd_w1, upd_b1, upd_w2, upd_b2):
        import jax, jax.numpy as jnp
        import numpy as np
        N_NODES = 5000
        N_EDGES = 80000
        ATOM_DIM = 128
        BOND_DIM = 64
        HIDDEN = 128
        row, col = (edge_index[0], edge_index[1])
        m_in = jnp.concatenate([x[row], edge_attr], axis=1)
        h = jax.nn.relu(m_in @ msg_w1 + msg_b1)
        messages = h @ msg_w2 + msg_b2
        aggregated = jax.ops.segment_sum(messages, col, num_segments=x.shape[0])
        u_in = jnp.concatenate([x, aggregated], axis=1)
        u = jax.nn.relu(u_in @ upd_w1 + upd_b1)
        updated_x = u @ upd_w2 + upd_b2
        return updated_x
    edge_index = jnp.stack([src, dst])
    h = jnp.maximum(_layernorm(x, axis=-1), 0.0)
    x = x + _L0_gnn_ref(h, edge_index, edge_attr_64, L0_gnn_msg_w1, L0_gnn_msg_b1, L0_gnn_msg_w2, L0_gnn_msg_b2, L0_gnn_upd_w1, L0_gnn_upd_b1, L0_gnn_upd_w2, L0_gnn_upd_b2)
    return x

_drawn_inputs = setup_inputs


def setup_inputs(seed=0):
    import zlib

    import numpy as np

    out = dict(_drawn_inputs(seed))
    spreads = {}
    factors = {'L0_gnn_upd_b1': 5.842}
    for name, (base, spread) in spreads.items():
        noise = np.random.default_rng([zlib.crc32(name.encode()), seed]).standard_normal(out[name].shape)
        drawn = base * np.exp(spread * noise) if base else spread * noise
        out[name] = jnp.asarray(drawn.astype(out[name].dtype))
    for name, factor in factors.items():
        out[name] = (out[name] * factor).astype(out[name].dtype)
    return out
```

```python
from contextlib import ExitStack

import concourse.bass as bass
from concourse import mybir

F32 = mybir.dt.float32
I32 = mybir.dt.int32
ALU = mybir.AluOpType
ACT = mybir.ActivationFunctionType
AX_X = mybir.AxisListType.X

P = 128
UNROLL = 5
TILES = 5
CHUNK = TILES * P
WINDOW = 128
WIDE = 512
ROWS = 4
EPS = 1e-5

BACK = [1, 3, 2, 2, 2]
CREDIT = 5


def gnn_layer(nc, x, src, dst_rows, dst_cols, attr, w_src, w_attr, b_msg1, w_msg2_t, b_msg2, w_node, w_agg, b_upd1,
              w_upd2, b_upd2, out):
    N, D = x.shape
    CHUNKS, K_ATTR, _ = attr.shape
    BODIES = CHUNKS // UNROLL
    NP = N // (ROWS * UNROLL * 5)
    J = N // NP
    GROUPS = J // ROWS
    GBODIES = GROUPS // UNROLL
    BLOCK = UNROLL * ROWS
    WINDOWS = -(-N // WIDE)
    PADDED = WINDOWS * WIDE
    CP = dst_rows.shape[0]
    assert D == P and CHUNKS % UNROLL == 0 and GROUPS % UNROLL == 0 and NP <= P and NP * J == N
    assert N - 1 + WINDOW <= PADDED and J * D <= PADDED and CP * UNROLL == CHUNKS

    table = nc.dram_tensor("table", (N, D), F32, kind="Internal").ap()
    ranges = nc.dram_tensor("ranges", (2, CHUNKS), F32, kind="Internal").ap()

    x_rows = x.rearrange("(p j) d -> p j d", j=J)
    out_rows = out.rearrange("(p j) d -> p j d", j=J)
    table_rows = table.rearrange("(p j) d -> p j d", j=J)

    with ExitStack() as ctx:
        def sb(name, shape, dt=F32):
            return ctx.enter_context(nc.sbuf_tensor(name, shape, dt))

        def ps(name, shape):
            return ctx.enter_context(nc.psum_tensor(name, shape, F32))

        def sem(name):
            return ctx.enter_context(nc.semaphore(name))

        w_src_sb = sb("w_src_sb", [D, D])
        w_attr_sb = sb("w_attr_sb", [K_ATTR, D])
        w_msg2_t_sb = sb("w_msg2_t_sb", [D, D])
        w_node_sb = sb("w_node_sb", [D, D])
        w_agg_sb = sb("w_agg_sb", [D, D])
        w_upd2_sb = sb("w_upd2_sb", [D, D])
        b_msg1_bc = sb("b_msg1_bc", [P, D])
        b_upd2_bc = sb("b_upd2_bc", [P, D])
        b_msg2_col = sb("b_msg2_col", [D, 1])
        b_upd1_col = sb("b_upd1_col", [D, 1])
        b_msg2_rep = sb("b_msg2_rep", [D, P])
        w_both = sb("w_both", [D, D])
        bias_both = sb("bias_both", [P, D])
        identity = sb("identity", [P, P])
        eps = sb("eps", [P, 1])
        iota_sb = sb("iota_sb", [P, WIDE])

        sums = sb("sums", [P, PADDED])
        update = sb("update", [P, PADDED])
        x_all = sums[0:NP, 0:J * D].rearrange("p (j d) -> p j d", d=D)

        dst_sb = sb("dst_sb", [P, CHUNKS, TILES], I32)
        dst_rel = sb("dst_rel", [P, CHUNKS, TILES])
        bounds = sb("bounds", [CP, 3, UNROLL])
        base_bc = sb("base_bc", [P, CHUNKS])
        span_row = sb("span_row", [1, CHUNKS])
        base_row = sb("base_row", [1, CHUNKS], I32)
        span_max = sb("span_max", [1, 1])
        span_int = sb("span_int", [1, 1], I32)
        rel = sb("rel", [P, TILES])

        index = sb("index", [P, UNROLL, TILES], I32)
        rows = sb("rows", [P, UNROLL, TILES, D])
        attrs = sb("attrs", [K_ATTR, UNROLL, CHUNK])
        hidden = sb("hidden", [P, UNROLL, TILES * D])
        masks = sb("masks", [P, TILES * WIDE])
        mask = masks[:, 0:2 * TILES * WINDOW].rearrange("p (k t w) -> p k t w", k=2, t=TILES)
        mask_wide = masks[:, :].rearrange("p (t w) -> p t w", t=TILES)
        dst_chunks = hidden[0:CP].rearrange("p k f -> p (k f)").bitcast(I32).rearrange("p (k f) -> p k f", k=UNROLL)

        stats = sb("stats", [NP, BLOCK, 6])
        mean_sum = sb("mean_sum", [NP, BLOCK])
        mean_gap = sb("mean_gap", [NP, BLOCK])
        squares = sb("squares", [NP, BLOCK])
        rstd = sb("rstd", [NP, J])
        shift = sb("shift", [NP, J])
        h = sb("h", [NP, 2, ROWS, D])
        h_t = sb("h_t", [P, 2, ROWS, NP])
        table_out = sb("table_out", [NP, UNROLL, ROWS, D])
        x_res = table_out

        pre = ps("pre", [P, 2, 1024])
        seg = ps("seg", [P, 2, 512])
        iota_ps = ps("iota_ps", [P, WIDE])
        setup_ps = ps("setup_ps", [P, 2, P])

        w_loaded = sem("w_loaded")
        dst_loaded = sem("dst_loaded")
        cols_loaded = sem("cols_loaded")
        x_loaded = [sem(f"x_loaded{k}") for k in range(UNROLL)]
        consts_made = sem("consts_made")
        iota_made = sem("iota_made")
        iota_moved = sem("iota_moved")
        prod_ready = sem("prod_ready")
        b_rep_made = sem("b_rep_made")
        both_made = sem("both_made")
        dve_step = sem("dve_step")
        bounds_made = sem("bounds_made")
        ranges_stored = sem("ranges_stored")
        base_loaded = sem("base_loaded")
        span_known = sem("span_known")
        stats_taken = sem("stats_taken")
        stats_made = sem("stats_made")
        halves_joined = sem("halves_joined")
        rstd_made = sem("rstd_made")
        deviation_made = sem("deviation_made")
        scales_made = sem("scales_made")
        h_made = sem("h_made")
        h_turned = sem("h_turned")
        h_t_made = sem("h_t_made")
        node_products = sem("node_products")
        table_made = sem("table_made")
        update_made = sem("update_made")
        table_stored = [sem(f"table_stored{k}") for k in range(UNROLL)]
        pool_turns = sem("pool_turns")
        act_turns = sem("act_turns")
        index_loaded = [sem(f"index_loaded{k}") for k in range(UNROLL)]
        attr_loaded = [sem(f"attr_loaded{k}") for k in range(UNROLL)]
        gathered = [sem(f"gathered{k}") for k in range(UNROLL)]
        pre_ready = sem("pre_ready")
        summed = sem("summed")
        relued = sem("relued")
        masks_made = sem("masks_made")
        seg_ready = sem("seg_ready")
        accumulated = sem("accumulated")
        rel_made = sem("rel_made")
        wide_masks = sem("wide_masks")
        wide_ready = sem("wide_ready")
        wide_added = sem("wide_added")
        sums_cleared = sem("sums_cleared")
        edges_done = sem("edges_done")
        res_loaded = [sem(f"res_loaded{k}") for k in range(UNROLL)]
        res_biased = sem("res_biased")
        u_ready = sem("u_ready")
        u_added = sem("u_added")
        u_relued = sem("u_relued")
        o_ready = sem("o_ready")
        o_made = sem("o_made")
        out_stored = [sem(f"out_stored{k}") for k in range(UNROLL)]

        W_LOADS = [(w_src_sb[:, :], w_src), (w_attr_sb[:, :], w_attr), (w_msg2_t_sb[:, :], w_msg2_t),
                   (w_node_sb[:, :], w_node), (w_agg_sb[:, :], w_agg), (w_upd2_sb[:, :], w_upd2),
                   (b_msg1_bc[:, :], b_msg1.to_broadcast([P, D])), (b_upd2_bc[:, :], b_upd2.to_broadcast([P, D])),
                   (b_msg2_col[:, :], b_msg2), (b_upd1_col[:, :], b_upd1)]

        block = ctx.enter_context(nc.Block())

        @block.sync
        def _(sp):
            def load_x(i, k):
                j = (i * UNROLL + k) * ROWS
                sp.dma_start(x_all[:, bass.ds(j, ROWS), :], x_rows[:, bass.ds(j, ROWS), :]).then_inc(x_loaded[k], 16)

            for k in range(UNROLL):
                load_x(0, k)
            sp.dma_start(dst_chunks, dst_rows).then_inc(dst_loaded, 16)
            with sp.Fori(1, GBODIES) as i:
                for k in range(UNROLL):
                    sp.wait_ge(x_loaded[k], i * 16)
                    load_x(i, k)
            sp.dma_start(dst_sb[:, :, :], dst_cols).then_inc(cols_loaded, 16)

            sp.wait_ge(bounds_made, 2)
            sp.dma_start(ranges[0].rearrange("(p k) -> p k", k=UNROLL), bounds[:, 0, :]).then_inc(ranges_stored, 16)
            sp.dma_start(ranges[1].rearrange("(p k) -> p k", k=UNROLL), bounds[:, 2, :]).then_inc(ranges_stored, 16)
            sp.wait_ge(ranges_stored, 32)
            sp.dma_start(base_bc[:, :], ranges[0:1, :].to_broadcast([P, CHUNKS])).then_inc(base_loaded, 16)
            sp.dma_start(span_row[:, :], ranges[1:2, :]).then_inc(base_loaded, 16)

            with sp.Fori(0, BODIES) as i:
                for k in range(UNROLL):
                    c = i * UNROLL + k
                    sp.wait_ge(summed, c + 1)
                    sp.dma_start(index[:, k, :], src[bass.ds(c, 1)].rearrange("a p t -> p (a t)"))\
                        .then_inc(index_loaded[k], 16)
                    sp.dma_start(attrs[:, k, :], attr[bass.ds(c, 1)].rearrange("a f e -> f (a e)"))\
                        .then_inc(attr_loaded[k], 16)

            def load_res(i, k):
                j = (i * UNROLL + k) * ROWS
                sp.dma_start(x_res[:, k], x_rows[:, bass.ds(j, ROWS), :]).then_inc(res_loaded[k], 16)

            for k in range(UNROLL):
                load_res(0, k)
            with sp.Fori(1, GBODIES) as i:
                for k in range(UNROLL):
                    sp.wait_ge(out_stored[k], i * 16)
                    load_res(i, k)

        @block.gpsimd
        def _(pool):
            pool.memset(identity[:, :], 1.0).then_inc(pool_turns, 1)
            pool.wait_ge(pool_turns, 1)
            pool.affine_select(out=identity[:, :], in_=identity[:, :], compare_op=ALU.is_equal, fill=0.0, base=0,
                               pattern=[[-1, P]], channel_multiplier=1).then_inc(consts_made, 1)
            pool.memset(eps[:, :], EPS).then_inc(consts_made, 1)
            pool.iota(iota_sb[:, :], pattern=[[1, WIDE]], base=0, channel_multiplier=0,
                      allow_small_or_imprecise_dtypes=True).then_inc(iota_made, 1)

            with pool.Fori(0, GBODIES) as i:
                for k in range(UNROLL):
                    g = i * UNROLL + k
                    pool.wait_ge(table_made, g + CREDIT + 1)
                    pool.sem_inc(pool_turns, 1)
                    pool.dma_start(table_rows[:, bass.ds(g * ROWS, ROWS), :], table_out[:, k]).then_inc(table_stored[k], 16)
            for k in range(UNROLL):
                pool.wait_ge(table_stored[k], 16 * GBODIES)

            with pool.Fori(0, BODIES) as i:
                for k in range(UNROLL):
                    pool.wait_ge(index_loaded[k], i * 16 + 16)
                    pool.sem_inc(pool_turns, 1)
                    for t in range(TILES):
                        pool.indirect_dma_start(rows[:, k, t, :], None, table,
                                                bass.IndirectOffsetOnAxis(index[:, k, t:t + 1], 0))\
                            .then_inc(gathered[k], 16)

            with pool.Fori(0, GBODIES) as i:
                for k in range(UNROLL):
                    pool.wait_ge(res_loaded[k], i * 16 + 16)
                    pool.tensor_tensor(x_res[:, k], x_res[:, k],
                                       b_upd2_bc[0:NP, :].unsqueeze(1).to_broadcast([NP, ROWS, D]), ALU.add)\
                        .then_inc(res_biased, 1)

        @block.tensor
        def _(pe):
            pe.wait_ge(w_loaded, 16 * len(W_LOADS))
            pe.matmul(setup_ps[:, 0, :], w_msg2_t_sb[:, :], w_agg_sb[:, :], start=True, stop=True).then_inc(prod_ready, 1)
            pe.wait_ge(b_rep_made, 1)
            pe.wait_ge(both_made, 1)
            pe.matmul(setup_ps[:, 1, :], b_msg2_rep[:, :], w_agg_sb[:, :], start=True, stop=True).then_inc(prod_ready, 1)

            def turn_h(g, k):
                pe.wait_ge(h_made, g + CREDIT + 1)
                pe.wait_ge(h_t_made, g + CREDIT + 1 - BACK[k])
                for r in range(ROWS):
                    last = pe.transpose(pre[:, k % 2, r * NP:(r + 1) * NP], h[:, k % 2, r, :], identity[0:NP, 0:NP])
                last.then_inc(h_turned, 1)

            def multiply_h(g, k):
                pe.wait_ge(h_t_made, g + CREDIT + 1)
                pe.wait_ge(table_made, g + CREDIT + 1 - BACK[k])
                pe.wait_ge(update_made, g + CREDIT + 1 - BACK[k])
                for r in range(ROWS):
                    pe.matmul(pre[0:NP, k % 2, 512 + r * D:512 + (r + 1) * D], h_t[:, k % 2, r, :], w_src_sb[:, :],
                              start=True, stop=True)
                pe.matmul(seg[:, k % 2, 0:ROWS * NP], w_node_sb[:, :], h_t[:, k % 2].rearrange("p r n -> p (r n)"),
                          start=True, stop=True).then_inc(node_products, 1)

            pe.wait_ge(consts_made, 2)
            with pe.Fori(0, GBODIES) as i:
                for k in range(UNROLL):
                    turn_h(i * UNROLL + k, k)
                    if k > 0:
                        multiply_h(i * UNROLL + k - 1, k - 1)
                multiply_h(i * UNROLL + UNROLL - 1, UNROLL - 1)

            def attr_products(i, k):
                pe.wait_ge(attr_loaded[k], i * 16 + 16)
                pe.wait_ge(summed, i * UNROLL + (k + CREDIT + 1 - BACK[k]))
                for t in range(TILES):
                    last = pe.matmul(pre[:, k % 2, t * D:(t + 1) * D], attrs[:, k, t * P:(t + 1) * P], w_attr_sb[:, :],
                                     start=True, stop=True)
                last.then_inc(pre_ready, 1)

            def segment_sums(i, k):
                pe.wait_ge(masks_made, i * UNROLL + (k + 1))
                pe.wait_ge(accumulated, i * UNROLL + (k + CREDIT + 1 - BACK[k]))
                for t in range(TILES):
                    pe.matmul(seg[:, k % 2, WINDOW:2 * WINDOW], bias_both[:, :], mask[:, k % 2, t, :],
                              start=(t == 0), stop=(t == TILES - 1))
                pe.wait_ge(relued, i * UNROLL + (k + 1))
                for t in range(TILES):
                    last = pe.matmul(seg[:, k % 2, 0:WINDOW], hidden[:, k, t * D:(t + 1) * D], mask[:, k % 2, t, :],
                                     start=(t == 0), stop=(t == TILES - 1))
                last.then_inc(seg_ready, 1)

            def wide_sums(i, k, w):
                pe.wait_ge(relued, i * UNROLL + (k + 1))
                pe.wait_ge(wide_masks, (i * UNROLL + k) * WINDOWS + w + 1)
                for t in range(TILES):
                    pe.matmul(seg[:, 0, :], hidden[:, k, t * D:(t + 1) * D], mask_wide[:, t, :], start=(t == 0), stop=(t == TILES - 1))
                for t in range(TILES):
                    last = pe.matmul(seg[:, 1, :], bias_both[:, :], mask_wide[:, t, :],
                                     start=(t == 0), stop=(t == TILES - 1))
                last.then_inc(wide_ready, 1)

            pe.wait_ge(both_made, 2)
            pe.wait_ge(span_known, 1)
            span = pe.value_load(span_int[0:1, 0:1], min_val=0, max_val=N)
            with pe.If(span < WINDOW):
                with pe.Fori(0, BODIES) as i:
                    for k in range(UNROLL):
                        attr_products(i, k)
                        if k > 0:
                            segment_sums(i, k - 1)
                    segment_sums(i, UNROLL - 1)
            with pe.Else():
                with pe.Fori(0, BODIES) as i:
                    for k in range(UNROLL):
                        attr_products(i, k)
                        with pe.Fori(0, WINDOWS) as w:
                            wide_sums(i, k, w)

            def update_products(g, k):
                pe.wait_ge(u_added, g + CREDIT + 1 - BACK[k])
                pe.matmul(seg[:, k % 2, 0:ROWS * NP], w_both[:, :],
                          sums[:, 0:N].rearrange("f (p j) -> f j p", j=J)[:, bass.ds(g * ROWS, ROWS), :],
                          start=True, stop=True).then_inc(u_ready, 1)

            def out_products(g, k):
                pe.wait_ge(u_relued, g + CREDIT + 1)
                pe.wait_ge(o_made, g + CREDIT + 1 - BACK[k])
                for r in range(ROWS):
                    last = pe.matmul(pre[0:NP, k % 2, r * D:(r + 1) * D], h_t[:, k % 2, r, :], w_upd2_sb[:, :],
                                     start=True, stop=True)
                last.then_inc(o_ready, 1)

            pe.wait_ge(edges_done, 1)
            with pe.Fori(0, GBODIES) as i:
                for k in range(UNROLL):
                    update_products(i * UNROLL + k, k)
                    if k > 0:
                        out_products(i * UNROLL + k - 1, k - 1)
                out_products(i * UNROLL + UNROLL - 1, UNROLL - 1)

        @block.scalar
        def _(act):
            for tile, source in W_LOADS:
                act.dma_start(tile, source).then_inc(w_loaded, 16)
            for credited in (h_made, u_relued, update_made, node_products, h_turned, seg_ready, o_ready):
                act.sem_inc(credited, CREDIT)
            act.wait_ge(w_loaded, 16 * len(W_LOADS))
            act.wait_ge(consts_made, 2)

            def deviation(i):
                act.wait_ge(stats_made, i + 1)
                act.sem_inc(act_turns, 1)
                j = i * BLOCK
                act.activation(rstd[:, bass.ds(j, BLOCK)], squares[:, :], ACT.Sqrt,
                               scale=1.0 / D, bias=eps[0:NP, :]).then_inc(deviation_made, 1)

            def normalise(g, k):
                act.wait_ge(h_turned, g + CREDIT + 1 - BACK[k])
                act.sem_inc(act_turns, 1)
                for r in range(ROWS):
                    j = g * ROWS + r
                    last = act.activation(h[:, k % 2, r, :], x_all[:, bass.ds(j, 1), :].rearrange("p a d -> p (a d)"),
                                          ACT.Relu, scale=rstd[:, bass.ds(j, 1)], bias=shift[:, bass.ds(j, 1)])
                last.then_inc(h_made, 1)

            def update_out(g, k):
                act.wait_ge(node_products, g + 1 + CREDIT)
                act.sem_inc(act_turns, 1)
                act.activation(update[:, 0:N].rearrange("f (p j) -> f j p", j=J)[:, bass.ds(g * ROWS, ROWS), :],
                               seg[:, k % 2, 0:ROWS * NP].rearrange("f (r p) -> f r p", r=ROWS), ACT.Identity,
                               bias=b_upd1_col[:, :]).then_inc(update_made, 1)

            def node_groups(i):
                act.wait_ge(scales_made, i + 1)
                act.sem_inc(act_turns, 1)
                for k in range(UNROLL):
                    normalise(i * UNROLL + k, k)
                    if k > 0:
                        update_out(i * UNROLL + k - 1, k - 1)
                update_out(i * UNROLL + UNROLL - 1, UNROLL - 1)

            deviation(0)
            with act.Fori(0, GBODIES - 1) as i:
                deviation(i + 1)
                node_groups(i)
            node_groups(GBODIES - 1)

            with act.Fori(0, BODIES) as i:
                for k in range(UNROLL):
                    act.wait_ge(summed, i * UNROLL + (k + CREDIT + 1))
                    act.activation(hidden[:, k, :], hidden[:, k, :], ACT.Relu).then_inc(relued, 1)

            def store(g, k):
                act.wait_ge(o_made, g + CREDIT + 1)
                act.dma_start(out_rows[:, bass.ds(g * ROWS, ROWS), :], x_res[:, k]).then_inc(out_stored[k], 16)

            with act.Fori(0, GBODIES) as i:
                for k in range(UNROLL):
                    act.wait_ge(u_added, i * UNROLL + (k + CREDIT + 1))
                    act.activation(h_t[:, k % 2], h_t[:, k % 2], ACT.Relu).then_inc(u_relued, 1)
                    if k > 0:
                        store(i * UNROLL + k - 1, k - 1)
                store(i * UNROLL + UNROLL - 1, UNROLL - 1)
            for k in range(UNROLL):
                act.wait_ge(out_stored[k], 16 * GBODIES)

        @block.vector
        def _(dve):
            for credited in (summed, accumulated, h_t_made, table_made, u_added, o_made):
                dve.sem_inc(credited, CREDIT)

            dve.memset(update[:, N:PADDED], 0.0)
            dve.wait_ge(dst_loaded, 16)
            dve.tensor_reduce(bounds[:, 0, :], dst_chunks, AX_X, ALU.min).then_inc(bounds_made, 1)
            dve.tensor_reduce(bounds[:, 1, :], dst_chunks, AX_X, ALU.max).then_inc(dve_step, 1)
            dve.wait_ge(bounds_made, 1)
            dve.wait_ge(dve_step, 1)
            dve.tensor_tensor(bounds[:, 2, :], bounds[:, 1, :], bounds[:, 0, :], ALU.subtract).then_inc(bounds_made, 1)

            def statistics(i):
                for k in range(UNROLL):
                    dve.wait_ge(x_loaded[k], i * 16 + 16)
                    for r in range(ROWS):
                        j = (i * UNROLL + k) * ROWS + r
                        last = dve.bn_stats(stats[:, k * ROWS + r, :],
                                            x_all[:, bass.ds(j, 1), :].rearrange("p a d -> p (a d)"))
                last.then_inc(stats_taken, 1)
                dve.wait_ge(stats_taken, i + 1)
                _, mean_e, squares_e, _, mean_o, squares_o = (stats[:, :, q] for q in range(6))
                dve.tensor_tensor(mean_sum[:, :], mean_e, mean_o, ALU.add).then_inc(halves_joined, 1)
                dve.tensor_tensor(mean_gap[:, :], mean_e, mean_o, ALU.subtract).then_inc(halves_joined, 1)
                dve.tensor_tensor(squares[:, :], squares_e, squares_o, ALU.add).then_inc(halves_joined, 1)
                dve.wait_ge(halves_joined, i * 4 + 3)
                dve.tensor_tensor(mean_gap[:, :], mean_gap[:, :], mean_gap[:, :], ALU.mult).then_inc(halves_joined, 1)
                dve.wait_ge(halves_joined, i * 4 + 4)
                dve.scalar_tensor_tensor(squares[:, :], mean_gap[:, :], D / 4.0, squares[:, :], ALU.mult, ALU.add)\
                    .then_inc(stats_made, 1)

            def scales(i):
                dve.wait_ge(deviation_made, i + 1)
                block = rstd[:, bass.ds(i * BLOCK, BLOCK)]
                dve.reciprocal(block, block).then_inc(rstd_made, 1)
                dve.wait_ge(rstd_made, i + 1)
                dve.scalar_tensor_tensor(shift[:, bass.ds(i * BLOCK, BLOCK)], mean_sum[:, :],
                                         -0.5, block, ALU.mult, ALU.mult).then_inc(scales_made, 1)

            def h_t_out(g, k):
                dve.wait_ge(h_turned, g + CREDIT + 1)
                dve.wait_ge(node_products, g + 1 + CREDIT - BACK[k])
                dve.tensor_copy(h_t[:, k % 2].rearrange("p r n -> p (r n)"), pre[:, k % 2, 0:ROWS * NP])\
                    .then_inc(h_t_made, 1)

            def table_rows_out(g, k):
                dve.wait_ge(node_products, g + 1 + CREDIT)
                dve.tensor_tensor(table_out[:, k], pre[0:NP, k % 2, 512:1024].rearrange("p (r d) -> p r d", r=ROWS),
                                  b_msg1_bc[0:NP, :].unsqueeze(1).to_broadcast([NP, ROWS, D]), ALU.add)\
                    .then_inc(table_made, 1)

            def node_groups(i, first):
                for k in range(UNROLL):
                    h_t_out(i * UNROLL + k, k)
                    if k > 0:
                        if not first:
                            dve.wait_ge(table_stored[k - 1], i * 16)
                        table_rows_out(i * UNROLL + k - 1, k - 1)
                if not first:
                    dve.wait_ge(table_stored[UNROLL - 1], i * 16)
                table_rows_out(i * UNROLL + UNROLL - 1, UNROLL - 1)

            statistics(0)
            scales(0)

            dve.wait_ge(w_loaded, 16 * len(W_LOADS))
            dve.tensor_copy(b_msg2_rep[:, :], b_msg2_col[:, 0:1].to_broadcast([D, P])).then_inc(b_rep_made, 1)
            dve.wait_ge(prod_ready, 1)
            dve.tensor_copy(w_both[:, :], setup_ps[:, 0, :]).then_inc(both_made, 1)
            dve.wait_ge(prod_ready, 2)
            dve.tensor_copy(bias_both[:, :], setup_ps[:, 1, :]).then_inc(both_made, 1)
            dve.wait_ge(iota_made, 1)
            dve.tensor_copy(iota_ps[:, :], iota_sb[:, :]).then_inc(iota_moved, 1)

            statistics(1)
            node_groups(0, True)
            scales(1)
            with dve.Fori(1, GBODIES - 1) as i:
                statistics(i + 1)
                node_groups(i, False)
                scales(i + 1)
            node_groups(GBODIES - 1, False)

            dve.wait_ge(base_loaded, 32)
            dve.tensor_copy(base_row[:, :], base_bc[0:1, :]).then_inc(dve_step, 1)
            dve.tensor_reduce(span_max[:, :], span_row[:, :], AX_X, ALU.max).then_inc(dve_step, 1)
            dve.wait_ge(dve_step, 3)
            dve.tensor_copy(span_int[:, :], span_max[:, :]).then_inc(span_known, 1)
            dve.wait_ge(h_made, GROUPS + CREDIT)
            dve.memset(sums[:, :], 0.0).then_inc(sums_cleared, 1)
            dve.wait_ge(cols_loaded, 16)
            dve.tensor_tensor(dst_rel[:, :, :], dst_sb[:, :, :],
                              base_bc[:, :].unsqueeze(2).to_broadcast([P, CHUNKS, TILES]), ALU.subtract)\
                .then_inc(dve_step, 1)

            def sum_rows(i, k):
                dve.wait_ge(gathered[k], i * (16 * TILES) + 16 * TILES)
                dve.wait_ge(pre_ready, i * UNROLL + (k + 1))
                dve.tensor_tensor(hidden[:, k, :], pre[:, k % 2, 0:TILES * D],
                                  rows[:, k].rearrange("p t d -> p (t d)"), ALU.add).then_inc(summed, 1)

            def make_masks(i, k):
                dve.wait_ge(seg_ready, i * UNROLL + (k + CREDIT + 1 - BACK[k]))
                c = i * UNROLL + k
                dve.tensor_tensor(mask[:, k % 2], iota_ps[:, 0:WINDOW].unsqueeze(1).to_broadcast([P, TILES, WINDOW]),
                                  dst_rel[:, bass.ds(c, 1), :].rearrange("p a t -> p (a t)").unsqueeze(2)
                                  .to_broadcast([P, TILES, WINDOW]), ALU.is_equal).then_inc(masks_made, 1)

            def accumulate(i, k):
                base = dve.value_load(base_row[0:1, bass.ds(i * UNROLL + k, 1)], min_val=0, max_val=N - 1)
                dve.wait_ge(seg_ready, i * UNROLL + (k + CREDIT + 1))
                dve.wait_ge(accumulated, i * UNROLL + (k + CREDIT))
                for total, part in ((sums, 0), (update, WINDOW)):
                    columns = total[:, bass.ds(base, WINDOW)]
                    last = dve.tensor_tensor(columns, seg[:, k % 2, part:part + WINDOW], columns, ALU.add)
                last.then_inc(accumulated, 1)

            def accumulate_wide(n, w):
                dve.wait_ge(wide_ready, n + 1)
                for total, part in ((sums, 0), (update, 1)):
                    columns = total[:, bass.ds(w * WIDE, WIDE)]
                    last = dve.tensor_tensor(columns, seg[:, part, :], columns, ALU.add)
                last.then_inc(wide_added, 1)

            dve.wait_ge(span_known, 1)
            dve.wait_ge(sums_cleared, 1)
            dve.wait_ge(iota_moved, 1)
            dve.wait_ge(dve_step, 4)
            dve.wait_ge(update_made, GROUPS + CREDIT)
            span = dve.value_load(span_int[0:1, 0:1], min_val=0, max_val=N)
            with dve.If(span < WINDOW):
                with dve.Fori(0, BODIES) as i:
                    for k in range(UNROLL):
                        make_masks(i, k)
                        sum_rows(i, k)
                        if k > 0:
                            accumulate(i, k - 1)
                    accumulate(i, UNROLL - 1)
            with dve.Else():
                with dve.Fori(0, BODIES) as i:
                    for k in range(UNROLL):
                        sum_rows(i, k)
                        c = i * UNROLL + k
                        dve.tensor_copy(rel[:, :], dst_sb[:, bass.ds(c, 1), :].rearrange("p a t -> p (a t)"))\
                            .then_inc(rel_made, 1)
                        with dve.Fori(0, WINDOWS) as w:
                            n = c * WINDOWS + w
                            dve.wait_ge(rel_made, n + c + 1)
                            dve.tensor_tensor(mask_wide, iota_ps[:, :].unsqueeze(1).to_broadcast([P, TILES, WIDE]),
                                              rel[:, :].unsqueeze(2).to_broadcast([P, TILES, WIDE]), ALU.is_equal)\
                                .then_inc(wide_masks, 1)
                            dve.wait_ge(wide_masks, n + 1)
                            dve.tensor_scalar(rel[:, :], rel[:, :], -float(WIDE), None, ALU.add).then_inc(rel_made, 1)
                            accumulate_wide(n, w)
                            dve.wait_ge(wide_added, n + 1)
            dve.drain().then_inc(edges_done, 1)

            def add_update(g, k):
                dve.wait_ge(u_ready, g + 1)
                dve.wait_ge(o_ready, g + CREDIT + 1 - BACK[k])
                dve.tensor_tensor(h_t[:, k % 2], seg[:, k % 2, 0:ROWS * NP].rearrange("f (r p) -> f r p", r=ROWS),
                                  update[:, 0:N].rearrange("f (p j) -> f j p", j=J)[:, bass.ds(g * ROWS, ROWS), :],
                                  ALU.add).then_inc(u_added, 1)

            def add_residual(g, k):
                dve.wait_ge(o_ready, g + CREDIT + 1)
                dve.wait_ge(res_biased, g + 1)
                dve.tensor_tensor(x_res[:, k], pre[0:NP, k % 2, 0:ROWS * D].rearrange("p (r d) -> p r d", r=ROWS),
                                  x_res[:, k], ALU.add).then_inc(o_made, 1)

            dve.wait_ge(edges_done, 1)
            with dve.Fori(0, GBODIES) as i:
                for k in range(UNROLL):
                    add_update(i * UNROLL + k, k)
                    if k > 0:
                        add_residual(i * UNROLL + k - 1, k - 1)
                add_residual(i * UNROLL + UNROLL - 1, UNROLL - 1)


def kernel(x, src, dst, edge_attr_64, L0_gnn_msg_w1, L0_gnn_msg_b1, L0_gnn_msg_w2, L0_gnn_msg_b2, L0_gnn_upd_w1,
           L0_gnn_upd_b1, L0_gnn_upd_w2, L0_gnn_upd_b2):
    import numpy as np
    import concourse.bacc as bacc
    from concourse.bass_utils import run_bass_kernel_spmd

    x, src, dst, attr = (np.asarray(a) for a in (x, src, dst, edge_attr_64))
    w1, b1, w2, b2 = (np.asarray(a) for a in (L0_gnn_msg_w1, L0_gnn_msg_b1, L0_gnn_msg_w2, L0_gnn_msg_b2))
    u1, ub1, u2, ub2 = (np.asarray(a) for a in (L0_gnn_upd_w1, L0_gnn_upd_b1, L0_gnn_upd_w2, L0_gnn_upd_b2))
    n, d = x.shape
    e, k_attr = attr.shape
    chunks = e // CHUNK
    arrays = {
        "x": x,
        "src": src.reshape(chunks, TILES, P).transpose(0, 2, 1),
        "dst_rows": dst.reshape(chunks // UNROLL, UNROLL, CHUNK),
        "dst_cols": dst.reshape(chunks, TILES, P).transpose(2, 0, 1),
        "attr": attr.reshape(chunks, CHUNK, k_attr).transpose(0, 2, 1),
        "w_src": w1[:d], "w_attr": w1[d:], "b_msg1": b1.reshape(1, d), "w_msg2_t": w2.T, "b_msg2": b2.reshape(d, 1),
        "w_node": u1[:d], "w_agg": u1[d:], "b_upd1": ub1.reshape(d, 1), "w_upd2": u2, "b_upd2": ub2.reshape(1, d),
    }
    nc = bacc.Bacc("TRN2", target_bir_lowering=False, num_devices=1)
    arrays = {"in_" + name: np.ascontiguousarray(a) for name, a in arrays.items()}
    args = {name[3:]: nc.dram_tensor(name, a.shape, mybir.dt.from_np(a.dtype), kind="ExternalInput").ap()
            for name, a in arrays.items()}
    out = nc.dram_tensor("out", (n, d), F32, kind="ExternalOutput").ap()
    gnn_layer(nc, out=out, **args)
    return run_bass_kernel_spmd(nc, [arrays], core_ids=[0]).results[0]["out"]
```

```python
from contextlib import ExitStack

import concourse.bass as bass
from concourse import mybir

F32 = mybir.dt.float32
I32 = mybir.dt.int32
ALU = mybir.AluOpType
ACT = mybir.ActivationFunctionType
AX_X = mybir.AxisListType.X

P = 128
UNROLL = 5
TILES = 5
CHUNK = TILES * P
WINDOW = 128
WIDE = 512
ROWS = 4
EPS = 1e-5

BACK = [1, 3, 2, 2, 2]
CREDIT = 5


def gnn_layer(nc, x, src, dst_rows, dst_cols, attr, w_src, w_attr, b_msg1, w_msg2_t, b_msg2, w_node, w_agg, b_upd1,
              w_upd2, b_upd2, out):
    N, D = x.shape
    CHUNKS, K_ATTR, _ = attr.shape
    BODIES = CHUNKS // UNROLL
    NP = N // (ROWS * UNROLL * 5)
    J = N // NP
    GROUPS = J // ROWS
    GBODIES = GROUPS // UNROLL
    BLOCK = UNROLL * ROWS
    WINDOWS = -(-N // WIDE)
    PADDED = WINDOWS * WIDE
    CP = dst_rows.shape[0]
    assert D == P and CHUNKS % UNROLL == 0 and GROUPS % UNROLL == 0 and NP <= P and NP * J == N
    assert N - 1 + WINDOW <= PADDED and J * D <= PADDED and CP * UNROLL == CHUNKS

    table = nc.dram_tensor("table", (N, D), F32, kind="Internal").ap()
    ranges = nc.dram_tensor("ranges", (2, CHUNKS), F32, kind="Internal").ap()

    x_rows = x.rearrange("(p j) d -> p j d", j=J)
    out_rows = out.rearrange("(p j) d -> p j d", j=J)
    table_rows = table.rearrange("(p j) d -> p j d", j=J)

    with ExitStack() as ctx:
        def sb(name, shape, dt=F32):
            return ctx.enter_context(nc.sbuf_tensor(name, shape, dt))

        def ps(name, shape):
            return ctx.enter_context(nc.psum_tensor(name, shape, F32))

        def sem(name):
            return ctx.enter_context(nc.semaphore(name))

        w_src_sb = sb("w_src_sb", [D, D])
        w_attr_sb = sb("w_attr_sb", [K_ATTR, D])
        w_msg2_t_sb = sb("w_msg2_t_sb", [D, D])
        w_node_sb = sb("w_node_sb", [D, D])
        w_agg_sb = sb("w_agg_sb", [D, D])
        w_upd2_sb = sb("w_upd2_sb", [D, D])
        b_msg1_bc = sb("b_msg1_bc", [P, D])
        b_upd2_bc = sb("b_upd2_bc", [P, D])
        b_msg2_col = sb("b_msg2_col", [D, 1])
        b_upd1_col = sb("b_upd1_col", [D, 1])
        b_msg2_rep = sb("b_msg2_rep", [D, P])
        w_both = sb("w_both", [D, D])
        bias_both = sb("bias_both", [P, D])
        identity = sb("identity", [P, P])
        eps = sb("eps", [P, 1])
        iota_sb = sb("iota_sb", [P, WIDE])

        sums = sb("sums", [P, PADDED])
        update = sb("update", [P, PADDED])
        x_all = sums[0:NP, 0:J * D].rearrange("p (j d) -> p j d", d=D)

        dst_sb = sb("dst_sb", [P, CHUNKS, TILES], I32)
        dst_rel = sb("dst_rel", [P, CHUNKS, TILES])
        bounds = sb("bounds", [CP, 3, UNROLL])
        base_bc = sb("base_bc", [P, CHUNKS])
        span_row = sb("span_row", [1, CHUNKS])
        base_row = sb("base_row", [1, CHUNKS], I32)
        span_max = sb("span_max", [1, 1])
        span_int = sb("span_int", [1, 1], I32)
        rel = sb("rel", [P, TILES])

        index = sb("index", [P, UNROLL, TILES], I32)
        rows = sb("rows", [P, UNROLL, TILES, D])
        attrs = sb("attrs", [K_ATTR, UNROLL, CHUNK])
        hidden = sb("hidden", [P, UNROLL, TILES * D])
        masks = sb("masks", [P, TILES * WIDE])
        mask = masks[:, 0:2 * TILES * WINDOW].rearrange("p (k t w) -> p k t w", k=2, t=TILES)
        mask_wide = masks[:, :].rearrange("p (t w) -> p t w", t=TILES)
        dst_chunks = hidden[0:CP].rearrange("p k f -> p (k f)").bitcast(I32).rearrange("p (k f) -> p k f", k=UNROLL)

        stats = sb("stats", [NP, BLOCK, 6])
        mean_sum = sb("mean_sum", [NP, BLOCK])
        mean_gap = sb("mean_gap", [NP, BLOCK])
        squares = sb("squares", [NP, BLOCK])
        rstd = sb("rstd", [NP, J])
        shift = sb("shift", [NP, J])
        table_out = sb("table_out", [NP, UNROLL, ROWS, D])
        x_res = table_out
        h = rows[0:NP, :, 0:ROWS, :]
        h_t = hidden[:, :, 0:ROWS * NP]
        u = h_t

        pre = ps("pre", [P, 2, 1024])
        seg = ps("seg", [P, 2, 512])
        iota_ps = ps("iota_ps", [P, WIDE])
        setup_ps = ps("setup_ps", [P, 2, P])
        bank = [pre[:, 0, 0:512], pre[:, 0, 512:1024], pre[:, 1, 0:512], pre[:, 1, 512:1024], iota_ps[:, :]]
        bank = [b[:, 0:ROWS * NP] for b in bank]

        w_loaded = sem("w_loaded")
        dst_loaded = sem("dst_loaded")
        cols_loaded = sem("cols_loaded")
        x_loaded = [sem(f"x_loaded{k}") for k in range(UNROLL)]
        consts_made = sem("consts_made")
        iota_made = sem("iota_made")
        iota_moved = sem("iota_moved")
        prod_ready = sem("prod_ready")
        b_rep_made = sem("b_rep_made")
        both_made = sem("both_made")
        dve_step = sem("dve_step")
        bounds_made = sem("bounds_made")
        ranges_stored = sem("ranges_stored")
        base_loaded = sem("base_loaded")
        span_known = sem("span_known")
        stats_taken = sem("stats_taken")
        stats_made = sem("stats_made")
        halves_joined = sem("halves_joined")
        rstd_made = sem("rstd_made")
        deviation_made = sem("deviation_made")
        scales_made = sem("scales_made")
        h_made = sem("h_made")
        h_turned = sem("h_turned")
        h_t_made = sem("h_t_made")
        table_ready = sem("table_ready")
        update_ready = sem("update_ready")
        table_made = sem("table_made")
        update_made = sem("update_made")
        table_stored = [sem(f"table_stored{k}") for k in range(UNROLL)]
        pool_turns = sem("pool_turns")
        act_turns = sem("act_turns")
        index_loaded = [sem(f"index_loaded{k}") for k in range(UNROLL)]
        attr_loaded = [sem(f"attr_loaded{k}") for k in range(UNROLL)]
        gathered = [sem(f"gathered{k}") for k in range(UNROLL)]
        pre_ready = sem("pre_ready")
        summed = sem("summed")
        relued = sem("relued")
        masks_made = sem("masks_made")
        seg_ready = sem("seg_ready")
        accumulated = sem("accumulated")
        rel_made = sem("rel_made")
        wide_masks = sem("wide_masks")
        wide_ready = sem("wide_ready")
        wide_added = sem("wide_added")
        sums_cleared = sem("sums_cleared")
        edges_done = sem("edges_done")
        res_loaded = [sem(f"res_loaded{k}") for k in range(UNROLL)]
        res_biased = sem("res_biased")
        u_ready = sem("u_ready")
        u_added = sem("u_added")
        u_relued = sem("u_relued")
        o_ready = sem("o_ready")
        o_made = sem("o_made")
        out_stored = [sem(f"out_stored{k}") for k in range(UNROLL)]

        W_LOADS = [(w_src_sb[:, :], w_src), (w_attr_sb[:, :], w_attr), (w_msg2_t_sb[:, :], w_msg2_t),
                   (w_node_sb[:, :], w_node), (w_agg_sb[:, :], w_agg), (w_upd2_sb[:, :], w_upd2),
                   (b_msg1_bc[:, :], b_msg1.to_broadcast([P, D])), (b_upd2_bc[:, :], b_upd2.to_broadcast([P, D])),
                   (b_msg2_col[:, :], b_msg2), (b_upd1_col[:, :], b_upd1)]

        block = ctx.enter_context(nc.Block())

        @block.sync
        def _(sp):
            def load_x(i, k):
                j = (i * UNROLL + k) * ROWS
                sp.dma_start(x_all[:, bass.ds(j, ROWS), :], x_rows[:, bass.ds(j, ROWS), :]).then_inc(x_loaded[k], 16)

            sp.dma_start(dst_chunks, dst_rows).then_inc(dst_loaded, 16)
            for k in range(UNROLL):
                load_x(0, k)
            with sp.Fori(1, GBODIES) as i:
                for k in range(UNROLL):
                    sp.wait_ge(x_loaded[k], i * 16)
                    load_x(i, k)
            sp.dma_start(dst_sb[:, :, :], dst_cols).then_inc(cols_loaded, 16)

            sp.wait_ge(bounds_made, 2)
            sp.dma_start(ranges[0].rearrange("(p k) -> p k", k=UNROLL), bounds[:, 0, :]).then_inc(ranges_stored, 16)
            sp.dma_start(ranges[1].rearrange("(p k) -> p k", k=UNROLL), bounds[:, 2, :]).then_inc(ranges_stored, 16)
            sp.wait_ge(ranges_stored, 32)
            sp.dma_start(base_bc[:, :], ranges[0:1, :].to_broadcast([P, CHUNKS])).then_inc(base_loaded, 16)
            sp.dma_start(span_row[:, :], ranges[1:2, :]).then_inc(base_loaded, 16)

            with sp.Fori(0, BODIES) as i:
                for k in range(UNROLL):
                    c = i * UNROLL + k
                    sp.wait_ge(summed, c + 1)
                    sp.dma_start(index[:, k, :], src[bass.ds(c, 1)].rearrange("a p t -> p (a t)"))\
                        .then_inc(index_loaded[k], 16)
                    sp.dma_start(attrs[:, k, :], attr[bass.ds(c, 1)].rearrange("a f e -> f (a e)"))\
                        .then_inc(attr_loaded[k], 16)

            def load_res(i, k):
                j = (i * UNROLL + k) * ROWS
                sp.dma_start(x_res[:, k], x_rows[:, bass.ds(j, ROWS), :]).then_inc(res_loaded[k], 16)

            for k in range(UNROLL):
                load_res(0, k)
            with sp.Fori(1, GBODIES) as i:
                for k in range(UNROLL):
                    sp.wait_ge(out_stored[k], i * 16)
                    load_res(i, k)

        @block.gpsimd
        def _(pool):
            pool.memset(identity[:, :], 1.0).then_inc(pool_turns, 1)
            pool.wait_ge(pool_turns, 1)
            pool.affine_select(out=identity[:, :], in_=identity[:, :], compare_op=ALU.is_equal, fill=0.0, base=0,
                               pattern=[[-1, P]], channel_multiplier=1).then_inc(consts_made, 1)
            pool.memset(eps[:, :], EPS).then_inc(consts_made, 1)
            pool.iota(iota_sb[:, :], pattern=[[1, WIDE]], base=0, channel_multiplier=0,
                      allow_small_or_imprecise_dtypes=True).then_inc(iota_made, 1)

            with pool.Fori(0, GBODIES) as i:
                for k in range(UNROLL):
                    g = i * UNROLL + k
                    pool.wait_ge(table_made, g + CREDIT + 1)
                    pool.sem_inc(pool_turns, 1)
                    pool.dma_start(table_rows[:, bass.ds(g * ROWS, ROWS), :], table_out[:, k]).then_inc(table_stored[k], 16)
            for k in range(UNROLL):
                pool.wait_ge(table_stored[k], 16 * GBODIES)

            with pool.Fori(0, BODIES) as i:
                for k in range(UNROLL):
                    pool.wait_ge(index_loaded[k], i * 16 + 16)
                    pool.sem_inc(pool_turns, 1)
                    for t in range(TILES):
                        pool.indirect_dma_start(rows[:, k, t, :], None, table,
                                                bass.IndirectOffsetOnAxis(index[:, k, t:t + 1], 0))\
                            .then_inc(gathered[k], 16)

            with pool.Fori(0, GBODIES) as i:
                for k in range(UNROLL):
                    pool.wait_ge(res_loaded[k], i * 16 + 16)
                    pool.tensor_tensor(x_res[:, k], x_res[:, k],
                                       b_upd2_bc[0:NP, :].unsqueeze(1).to_broadcast([NP, ROWS, D]), ALU.add)\
                        .then_inc(res_biased, 1)

        @block.tensor
        def _(pe):
            pe.wait_ge(w_loaded, 16 * len(W_LOADS))
            pe.wait_ge(consts_made, 2)

            def turn_h(g, k):
                pe.wait_ge(h_made, g + CREDIT + 1)
                pe.wait_ge(h_t_made, g + CREDIT + 1 - BACK[k])
                for r in range(ROWS):
                    last = pe.transpose(pre[:, k % 2, r * NP:(r + 1) * NP], h[:, k, r, :], identity[0:NP, 0:NP])
                last.then_inc(h_turned, 1)

            def node_products(g, k):
                pe.wait_ge(h_t_made, g + CREDIT + 1)
                pe.wait_ge(table_made, g + CREDIT + 1 - BACK[k])
                for r in range(ROWS):
                    last = pe.matmul(seg[0:NP, k % 2, r * D:(r + 1) * D], h_t[:, k, r * NP:(r + 1) * NP],
                                     w_src_sb[:, :], start=True, stop=True)
                last.then_inc(table_ready, 1)
                pe.wait_ge(update_made, g + CREDIT + 1 - BACK[k])
                pe.matmul(pre[:, k % 2, 512:512 + ROWS * NP], w_node_sb[:, :], h_t[:, k, :],
                          start=True, stop=True).then_inc(update_ready, 1)

            def node_groups(i, last):
                for k in range(UNROLL):
                    if not last or k + 1 < UNROLL:
                        turn_h(i * UNROLL + (k + 1), (k + 1) % UNROLL)
                    node_products(i * UNROLL + k, k)

            turn_h(0, 0)
            with pe.Fori(0, GBODIES - 1) as i:
                node_groups(i, False)
            node_groups(GBODIES - 1, True)

            pe.wait_ge(b_rep_made, 1)
            pe.matmul(setup_ps[:, 0, :], w_msg2_t_sb[:, :], w_agg_sb[:, :], start=True, stop=True)
            pe.matmul(setup_ps[:, 1, :], b_msg2_rep[:, :], w_agg_sb[:, :], start=True, stop=True).then_inc(prod_ready, 1)

            def attr_products(i, k):
                pe.wait_ge(attr_loaded[k], i * 16 + 16)
                pe.wait_ge(summed, i * UNROLL + (k + CREDIT + 1 - BACK[k]))
                for t in range(TILES):
                    last = pe.matmul(pre[:, k % 2, t * D:(t + 1) * D], attrs[:, k, t * P:(t + 1) * P], w_attr_sb[:, :],
                                     start=True, stop=True)
                last.then_inc(pre_ready, 1)

            def segment_sums(i, k):
                pe.wait_ge(masks_made, i * UNROLL + (k + 1))
                pe.wait_ge(accumulated, i * UNROLL + (k + CREDIT + 1 - BACK[k]))
                for t in range(TILES):
                    pe.matmul(seg[:, k % 2, WINDOW:2 * WINDOW], bias_both[:, :], mask[:, k % 2, t, :],
                              start=(t == 0), stop=(t == TILES - 1))
                pe.wait_ge(relued, i * UNROLL + (k + 1))
                for t in range(TILES):
                    last = pe.matmul(seg[:, k % 2, 0:WINDOW], hidden[:, k, t * D:(t + 1) * D], mask[:, k % 2, t, :],
                                     start=(t == 0), stop=(t == TILES - 1))
                last.then_inc(seg_ready, 1)

            def wide_sums(i, k, w):
                pe.wait_ge(relued, i * UNROLL + (k + 1))
                pe.wait_ge(wide_masks, (i * UNROLL + k) * WINDOWS + w + 1)
                for t in range(TILES):
                    pe.matmul(seg[:, 0, :], hidden[:, k, t * D:(t + 1) * D], mask_wide[:, t, :], start=(t == 0), stop=(t == TILES - 1))
                for t in range(TILES):
                    last = pe.matmul(seg[:, 1, :], bias_both[:, :], mask_wide[:, t, :],
                                     start=(t == 0), stop=(t == TILES - 1))
                last.then_inc(wide_ready, 1)

            pe.wait_ge(both_made, 2)
            pe.wait_ge(update_made, GROUPS + CREDIT)
            pe.wait_ge(span_known, 1)
            span = pe.value_load(span_int[0:1, 0:1], min_val=0, max_val=N)
            with pe.If(span < WINDOW):
                with pe.Fori(0, BODIES) as i:
                    for k in range(UNROLL):
                        attr_products(i, k)
                        if k > 0:
                            segment_sums(i, k - 1)
                    segment_sums(i, UNROLL - 1)
            with pe.Else():
                with pe.Fori(0, BODIES) as i:
                    for k in range(UNROLL):
                        attr_products(i, k)
                        with pe.Fori(0, WINDOWS) as w:
                            wide_sums(i, k, w)

            def update_products(g, k):
                pe.wait_ge(u_added, g + 1)
                pe.matmul(bank[k], w_both[:, :],
                          sums[:, 0:N].rearrange("f (p j) -> f j p", j=J)[:, bass.ds(g * ROWS, ROWS), :],
                          start=True, stop=True).then_inc(u_ready, 1)

            def out_products(g, k):
                pe.wait_ge(u_relued, g + CREDIT + 1)
                pe.wait_ge(o_made, g + CREDIT + 1 - BACK[k])
                for r in range(ROWS):
                    last = pe.matmul(seg[0:NP, k % 2, r * D:(r + 1) * D], u[:, k, r * NP:(r + 1) * NP], w_upd2_sb[:, :],
                                     start=True, stop=True)
                last.then_inc(o_ready, 1)

            def out_groups(i, last):
                for k in range(UNROLL):
                    if not last or k + 2 < UNROLL:
                        update_products(i * UNROLL + (k + 2), (k + 2) % UNROLL)
                    out_products(i * UNROLL + k, k)

            pe.wait_ge(edges_done, 1)
            update_products(0, 0)
            update_products(1, 1)
            with pe.Fori(0, GBODIES - 1) as i:
                out_groups(i, False)
            out_groups(GBODIES - 1, True)

        @block.scalar
        def _(act):
            for tile, source in W_LOADS:
                act.dma_start(tile, source).then_inc(w_loaded, 16)
            for credited in (h_made, u_relued, update_made, update_ready, h_turned, seg_ready, o_ready):
                act.sem_inc(credited, CREDIT)
            act.wait_ge(w_loaded, 16 * len(W_LOADS))
            act.wait_ge(consts_made, 2)

            def deviation(i):
                act.wait_ge(stats_made, i + 1)
                act.sem_inc(act_turns, 1)
                j = i * BLOCK
                act.activation(rstd[:, bass.ds(j, BLOCK)], squares[:, :], ACT.Sqrt,
                               scale=1.0 / D, bias=eps[0:NP, :]).then_inc(deviation_made, 1)

            def normalise(g, k):
                act.wait_ge(h_turned, g + 1)
                act.sem_inc(act_turns, 1)
                for r in range(ROWS):
                    j = g * ROWS + r
                    last = act.activation(h[:, k, r, :], x_all[:, bass.ds(j, 1), :].rearrange("p a d -> p (a d)"),
                                          ACT.Relu, scale=rstd[:, bass.ds(j, 1)], bias=shift[:, bass.ds(j, 1)])
                last.then_inc(h_made, 1)

            def update_out(g, k):
                act.wait_ge(update_ready, g + CREDIT + 1)
                act.sem_inc(act_turns, 1)
                act.activation(update[:, 0:N].rearrange("f (p j) -> f j p", j=J)[:, bass.ds(g * ROWS, ROWS), :],
                               pre[:, k % 2, 512:512 + ROWS * NP].rearrange("f (r p) -> f r p", r=ROWS), ACT.Identity,
                               bias=b_upd1_col[:, :]).then_inc(update_made, 1)

            def node_groups(i, last):
                for k in range(UNROLL):
                    if not last or k + 2 < UNROLL:
                        if k + 2 == UNROLL:
                            act.wait_ge(scales_made, i + 2)
                            act.sem_inc(act_turns, 1)
                        normalise(i * UNROLL + (k + 2), (k + 2) % UNROLL)
                    if not last and k == 1:
                        deviation(i + 1)
                    update_out(i * UNROLL + k, k)

            deviation(0)
            act.wait_ge(scales_made, 1)
            normalise(0, 0)
            normalise(1, 1)
            with act.Fori(0, GBODIES - 1) as i:
                node_groups(i, False)
            node_groups(GBODIES - 1, True)

            with act.Fori(0, BODIES) as i:
                for k in range(UNROLL):
                    act.wait_ge(summed, i * UNROLL + (k + CREDIT + 1))
                    act.activation(hidden[:, k, :], hidden[:, k, :], ACT.Relu).then_inc(relued, 1)

            def store(g, k):
                act.wait_ge(o_made, g + CREDIT + 1)
                act.dma_start(out_rows[:, bass.ds(g * ROWS, ROWS), :], x_res[:, k]).then_inc(out_stored[k], 16)

            def relu_u(g, k):
                act.wait_ge(u_added, g + CREDIT + 1)
                act.activation(u[:, k], u[:, k], ACT.Relu).then_inc(u_relued, 1)

            def out_groups(i, last):
                for k in range(UNROLL):
                    if not last or k + 1 < UNROLL:
                        relu_u(i * UNROLL + (k + 1), (k + 1) % UNROLL)
                    store(i * UNROLL + k, k)

            relu_u(0, 0)
            with act.Fori(0, GBODIES - 1) as i:
                out_groups(i, False)
            out_groups(GBODIES - 1, True)
            for k in range(UNROLL):
                act.wait_ge(out_stored[k], 16 * GBODIES)

        @block.vector
        def _(dve):
            for credited in (summed, accumulated, h_t_made, table_made, u_added, o_made):
                dve.sem_inc(credited, CREDIT)

            dve.memset(update[:, N:PADDED], 0.0)
            dve.wait_ge(dst_loaded, 16)
            dve.tensor_reduce(bounds[:, 0, :], dst_chunks, AX_X, ALU.min).then_inc(bounds_made, 1)
            dve.tensor_reduce(bounds[:, 1, :], dst_chunks, AX_X, ALU.max).then_inc(dve_step, 1)
            dve.wait_ge(bounds_made, 1)
            dve.wait_ge(dve_step, 1)
            dve.tensor_tensor(bounds[:, 2, :], bounds[:, 1, :], bounds[:, 0, :], ALU.subtract).then_inc(bounds_made, 1)

            def statistics(i, k):
                dve.wait_ge(x_loaded[k], i * 16 + 16)
                for r in range(ROWS):
                    j = (i * UNROLL + k) * ROWS + r
                    last = dve.bn_stats(stats[:, k * ROWS + r, :],
                                        x_all[:, bass.ds(j, 1), :].rearrange("p a d -> p (a d)"))
                last.then_inc(stats_taken, 1)

            def join_statistics(i):
                dve.wait_ge(stats_taken, i * UNROLL + UNROLL)
                _, mean_e, squares_e, _, mean_o, squares_o = (stats[:, :, q] for q in range(6))
                dve.tensor_tensor(mean_sum[:, :], mean_e, mean_o, ALU.add).then_inc(halves_joined, 1)
                dve.tensor_tensor(mean_gap[:, :], mean_e, mean_o, ALU.subtract).then_inc(halves_joined, 1)
                dve.tensor_tensor(squares[:, :], squares_e, squares_o, ALU.add).then_inc(halves_joined, 1)
                dve.wait_ge(halves_joined, i * 4 + 3)
                dve.tensor_tensor(mean_gap[:, :], mean_gap[:, :], mean_gap[:, :], ALU.mult).then_inc(halves_joined, 1)
                dve.wait_ge(halves_joined, i * 4 + 4)
                dve.scalar_tensor_tensor(squares[:, :], mean_gap[:, :], D / 4.0, squares[:, :], ALU.mult, ALU.add)\
                    .then_inc(stats_made, 1)

            def scales(i):
                dve.wait_ge(deviation_made, i + 1)
                block = rstd[:, bass.ds(i * BLOCK, BLOCK)]
                dve.reciprocal(block, block).then_inc(rstd_made, 1)
                dve.wait_ge(rstd_made, i + 1)
                dve.scalar_tensor_tensor(shift[:, bass.ds(i * BLOCK, BLOCK)], mean_sum[:, :], -0.5, block,
                                         ALU.mult, ALU.mult).then_inc(scales_made, 1)

            def h_t_out(g, k):
                dve.wait_ge(h_turned, g + CREDIT + 1)
                dve.wait_ge(update_ready, g + 1)
                dve.tensor_copy(h_t[:, k, :], pre[:, k % 2, 0:ROWS * NP]).then_inc(h_t_made, 1)

            def table_rows_out(i, k, first):
                if not first:
                    dve.wait_ge(table_stored[k], i * 16)
                dve.wait_ge(table_ready, i * UNROLL + (k + 1))
                dve.tensor_tensor(table_out[:, k], seg[0:NP, k % 2, :].rearrange("p (r d) -> p r d", r=ROWS),
                                  b_msg1_bc[0:NP, :].unsqueeze(1).to_broadcast([NP, ROWS, D]), ALU.add)\
                    .then_inc(table_made, 1)

            def node_groups(i, first, last):
                between = {0: (0, 1, 2), 1: (3, 4)}
                for k in range(UNROLL):
                    if not last or k + 1 < UNROLL:
                        h_t_out(i * UNROLL + (k + 1), (k + 1) % UNROLL)
                    if not last:
                        for s in between.get(k, ()):
                            statistics(i + 1, s)
                        if k == 1:
                            join_statistics(i + 1)
                        if k == 2:
                            scales(i + 1)
                    table_rows_out(i, k, first)

            for k in range(UNROLL):
                statistics(0, k)
            join_statistics(0)
            scales(0)
            dve.wait_ge(w_loaded, 16 * len(W_LOADS))
            h_t_out(0, 0)
            node_groups(0, True, False)
            with dve.Fori(1, GBODIES - 1) as i:
                node_groups(i, False, False)
            node_groups(GBODIES - 1, False, True)

            dve.tensor_copy(b_msg2_rep[:, :], b_msg2_col[:, 0:1].to_broadcast([D, P])).then_inc(b_rep_made, 1)
            dve.wait_ge(base_loaded, 32)
            dve.tensor_copy(base_row[:, :], base_bc[0:1, :]).then_inc(dve_step, 1)
            dve.tensor_reduce(span_max[:, :], span_row[:, :], AX_X, ALU.max).then_inc(dve_step, 1)
            dve.wait_ge(dve_step, 3)
            dve.tensor_copy(span_int[:, :], span_max[:, :]).then_inc(span_known, 1)
            dve.wait_ge(h_made, GROUPS + CREDIT)
            dve.memset(sums[:, :], 0.0).then_inc(sums_cleared, 1)
            dve.wait_ge(cols_loaded, 16)
            dve.tensor_tensor(dst_rel[:, :, :], dst_sb[:, :, :],
                              base_bc[:, :].unsqueeze(2).to_broadcast([P, CHUNKS, TILES]), ALU.subtract)\
                .then_inc(dve_step, 1)

            def sum_rows(i, k):
                dve.wait_ge(gathered[k], i * (16 * TILES) + 16 * TILES)
                dve.wait_ge(pre_ready, i * UNROLL + (k + 1))
                dve.tensor_tensor(hidden[:, k, :], pre[:, k % 2, 0:TILES * D],
                                  rows[:, k].rearrange("p t d -> p (t d)"), ALU.add).then_inc(summed, 1)

            def make_masks(i, k):
                dve.wait_ge(seg_ready, i * UNROLL + (k + CREDIT + 1 - BACK[k]))
                c = i * UNROLL + k
                dve.tensor_tensor(mask[:, k % 2], iota_ps[:, 0:WINDOW].unsqueeze(1).to_broadcast([P, TILES, WINDOW]),
                                  dst_rel[:, bass.ds(c, 1), :].rearrange("p a t -> p (a t)").unsqueeze(2)
                                  .to_broadcast([P, TILES, WINDOW]), ALU.is_equal).then_inc(masks_made, 1)

            def accumulate(i, k):
                base = dve.value_load(base_row[0:1, bass.ds(i * UNROLL + k, 1)], min_val=0, max_val=N - 1)
                dve.wait_ge(seg_ready, i * UNROLL + (k + CREDIT + 1))
                dve.wait_ge(accumulated, i * UNROLL + (k + CREDIT))
                for total, part in ((sums, 0), (update, WINDOW)):
                    columns = total[:, bass.ds(base, WINDOW)]
                    last = dve.tensor_tensor(columns, seg[:, k % 2, part:part + WINDOW], columns, ALU.add)
                last.then_inc(accumulated, 1)

            def accumulate_wide(n, w):
                dve.wait_ge(wide_ready, n + 1)
                for total, part in ((sums, 0), (update, 1)):
                    columns = total[:, bass.ds(w * WIDE, WIDE)]
                    last = dve.tensor_tensor(columns, seg[:, part, :], columns, ALU.add)
                last.then_inc(wide_added, 1)

            dve.wait_ge(prod_ready, 1)
            dve.tensor_copy(w_both[:, :], setup_ps[:, 0, :]).then_inc(both_made, 1)
            dve.tensor_copy(bias_both[:, :], setup_ps[:, 1, :]).then_inc(both_made, 1)
            dve.wait_ge(update_made, GROUPS + CREDIT)
            dve.wait_ge(iota_made, 1)
            dve.tensor_copy(iota_ps[:, :], iota_sb[:, :]).then_inc(iota_moved, 1)
            dve.wait_ge(span_known, 1)
            dve.wait_ge(sums_cleared, 1)
            dve.wait_ge(iota_moved, 1)
            dve.wait_ge(dve_step, 4)
            span = dve.value_load(span_int[0:1, 0:1], min_val=0, max_val=N)
            with dve.If(span < WINDOW):
                with dve.Fori(0, BODIES) as i:
                    for k in range(UNROLL):
                        make_masks(i, k)
                        sum_rows(i, k)
                        if k > 0:
                            accumulate(i, k - 1)
                    accumulate(i, UNROLL - 1)
            with dve.Else():
                with dve.Fori(0, BODIES) as i:
                    for k in range(UNROLL):
                        sum_rows(i, k)
                        c = i * UNROLL + k
                        dve.tensor_copy(rel[:, :], dst_sb[:, bass.ds(c, 1), :].rearrange("p a t -> p (a t)"))\
                            .then_inc(rel_made, 1)
                        with dve.Fori(0, WINDOWS) as w:
                            n = c * WINDOWS + w
                            dve.wait_ge(rel_made, n + c + 1)
                            dve.tensor_tensor(mask_wide, iota_ps[:, :].unsqueeze(1).to_broadcast([P, TILES, WIDE]),
                                              rel[:, :].unsqueeze(2).to_broadcast([P, TILES, WIDE]), ALU.is_equal)\
                                .then_inc(wide_masks, 1)
                            dve.wait_ge(wide_masks, n + 1)
                            dve.tensor_scalar(rel[:, :], rel[:, :], -float(WIDE), None, ALU.add).then_inc(rel_made, 1)
                            accumulate_wide(n, w)
                            dve.wait_ge(wide_added, n + 1)
            dve.drain().then_inc(edges_done, 1)

            def add_update(g, k):
                dve.wait_ge(u_ready, g + 1)
                dve.wait_ge(o_ready, g + 1)
                dve.tensor_tensor(u[:, k].rearrange("f (r p) -> f r p", r=ROWS),
                                  bank[k].rearrange("f (r p) -> f r p", r=ROWS),
                                  update[:, 0:N].rearrange("f (p j) -> f j p", j=J)[:, bass.ds(g * ROWS, ROWS), :],
                                  ALU.add).then_inc(u_added, 1)

            def add_residual(g, k):
                dve.wait_ge(o_ready, g + CREDIT + 1)
                dve.wait_ge(res_biased, g + 1)
                dve.tensor_tensor(x_res[:, k], seg[0:NP, k % 2, :].rearrange("p (r d) -> p r d", r=ROWS),
                                  x_res[:, k], ALU.add).then_inc(o_made, 1)

            def out_groups(i, last):
                for k in range(UNROLL):
                    if not last or k + 1 < UNROLL:
                        add_update(i * UNROLL + (k + 1), (k + 1) % UNROLL)
                    add_residual(i * UNROLL + k, k)

            add_update(0, 0)
            with dve.Fori(0, GBODIES - 1) as i:
                out_groups(i, False)
            out_groups(GBODIES - 1, True)


def kernel(x, src, dst, edge_attr_64, L0_gnn_msg_w1, L0_gnn_msg_b1, L0_gnn_msg_w2, L0_gnn_msg_b2, L0_gnn_upd_w1,
           L0_gnn_upd_b1, L0_gnn_upd_w2, L0_gnn_upd_b2):
    import numpy as np
    import concourse.bacc as bacc
    from concourse.bass_utils import run_bass_kernel_spmd

    x, src, dst, attr = (np.asarray(a) for a in (x, src, dst, edge_attr_64))
    w1, b1, w2, b2 = (np.asarray(a) for a in (L0_gnn_msg_w1, L0_gnn_msg_b1, L0_gnn_msg_w2, L0_gnn_msg_b2))
    u1, ub1, u2, ub2 = (np.asarray(a) for a in (L0_gnn_upd_w1, L0_gnn_upd_b1, L0_gnn_upd_w2, L0_gnn_upd_b2))
    n, d = x.shape
    e, k_attr = attr.shape
    chunks = e // CHUNK
    arrays = {
        "x": x,
        "src": src.reshape(chunks, TILES, P).transpose(0, 2, 1),
        "dst_rows": dst.reshape(chunks // UNROLL, UNROLL, CHUNK),
        "dst_cols": dst.reshape(chunks, TILES, P).transpose(2, 0, 1),
        "attr": attr.reshape(chunks, CHUNK, k_attr).transpose(0, 2, 1),
        "w_src": w1[:d], "w_attr": w1[d:], "b_msg1": b1.reshape(1, d), "w_msg2_t": w2.T, "b_msg2": b2.reshape(d, 1),
        "w_node": u1[:d], "w_agg": u1[d:], "b_upd1": ub1.reshape(d, 1), "w_upd2": u2, "b_upd2": ub2.reshape(1, d),
    }
    nc = bacc.Bacc("TRN2", target_bir_lowering=False, num_devices=1)
    arrays = {"in_" + name: np.ascontiguousarray(a) for name, a in arrays.items()}
    args = {name[3:]: nc.dram_tensor(name, a.shape, mybir.dt.from_np(a.dtype), kind="ExternalInput").ap()
            for name, a in arrays.items()}
    out = nc.dram_tensor("out", (n, d), F32, kind="ExternalOutput").ap()
    gnn_layer(nc, out=out, **args)
    return run_bass_kernel_spmd(nc, [arrays], core_ids=[0]).results[0]["out"]
```

```python
from contextlib import ExitStack

import concourse.bass as bass
from concourse import mybir

F32 = mybir.dt.float32
I32 = mybir.dt.int32
ALU = mybir.AluOpType
ACT = mybir.ActivationFunctionType
AX_X = mybir.AxisListType.X

P = 128
UNROLL = 5
TILES = 5
CHUNK = TILES * P
WINDOW = 128
WIDE = 256
EARLY = 15
ROWS = 4
EPS = 1e-5

BACK = [1, 2, 2, 2, 2, 2]
BACK_AFTER_SIX = [2, 2, 2, 2, 2, 2]
PAIR = 2 * UNROLL + 1
CREDIT = 6


def after(step, back=0):
    return step + (CREDIT + 1 - back)


def gnn_layer(nc, x, src, dst_rows, dst_cols, attr, w_src, w_attr, b_msg1, w_msg2_t, b_msg2, w_node, w_agg, b_upd1,
              w_upd2, b_upd2, out):
    N, D = x.shape
    CHUNKS, K_ATTR, _ = attr.shape
    BODIES = (CHUNKS - EARLY) // UNROLL
    NP = N // (ROWS * UNROLL * 5)
    J = N // NP
    GROUPS = J // ROWS
    GBODIES = GROUPS // UNROLL
    BLOCK = UNROLL * ROWS
    WINDOWS = -(-N // WIDE)
    PADDED = max(WINDOWS * WIDE, N - 1 + WINDOW)
    CP = dst_rows.shape[0]
    CUT, CUT_DST = ([(0, n // 16 * 16), (n // 16 * 16, n)] for n in (NP, CP))
    assert D == P and CHUNKS % UNROLL == 0 and EARLY % UNROLL == 0 and CP * UNROLL == CHUNKS
    assert 2 * EARLY + GROUPS < BODIES and N <= 2 ** 24
    assert GROUPS % UNROLL == 0 and GBODIES > 3 and NP <= P and NP * J == N

    table = nc.dram_tensor("table", (N, D), F32, kind="Internal").ap()
    ranges = nc.dram_tensor("ranges", (2, CHUNKS), F32, kind="Internal").ap()

    x_rows = x.rearrange("(p j) d -> p j d", j=J)
    out_rows = out.rearrange("(p j) d -> p j d", j=J)
    table_rows = table.rearrange("(p j) d -> p j d", j=J)

    with ExitStack() as ctx:
        def sb(name, shape, dt=F32):
            return ctx.enter_context(nc.sbuf_tensor(name, shape, dt))

        def ps(name, shape):
            return ctx.enter_context(nc.psum_tensor(name, shape, F32))

        def sem(name):
            return ctx.enter_context(nc.semaphore(name))

        w_src_sb = sb("w_src_sb", [D, D])
        w_attr_sb = sb("w_attr_sb", [2 * K_ATTR, D])
        w_msg2_t_sb = sb("w_msg2_t_sb", [D, D])
        w_node_sb = sb("w_node_sb", [D, D])
        w_agg_sb = sb("w_agg_sb", [D, D])
        w_upd2_sb = sb("w_upd2_sb", [D, D])
        b_msg1_bc = sb("b_msg1_bc", [P, D])
        b_upd2_bc = sb("b_upd2_bc", [P, D])
        b_msg2_col = sb("b_msg2_col", [D, 1])
        b_upd1_col = sb("b_upd1_col", [D, 1])
        b_msg2_rep = sb("b_msg2_rep", [D, P])
        w_both = w_msg2_t_sb
        bias_both = b_msg2_rep
        identity = sb("identity", [P, P])
        eps = sb("eps", [P, 1])

        x_all = sb("x_all", [NP, J, D])
        update = sb("update", [P, PADDED])

        dst_rel = sb("dst_rel", [P, CHUNKS, TILES])
        dst_sb = dst_rel[:, :, :].bitcast(I32)
        bounds = sb("bounds", [CP, 3, UNROLL])
        base_bc = sb("base_bc", [P, CHUNKS])
        span_max = sb("span_max", [1, 1])
        span_int = sb("span_int", [1, 1], I32)
        rel = sb("rel", [P, TILES])

        index = sb("index", [P, UNROLL, TILES], I32)
        rows = sb("rows", [P, UNROLL, TILES, D])
        attr_space = sb("attr_space", [2 * K_ATTR, UNROLL * CHUNK])
        attrs = attr_space[0:K_ATTR, :].rearrange("f (k e) -> f k e", k=UNROLL)
        attrs_early = attr_space[K_ATTR:2 * K_ATTR, 0:CHUNK]
        span_row = attr_space[K_ATTR:K_ATTR + 1, CHUNK:CHUNK + CHUNKS]
        base_row = attr_space[K_ATTR:K_ATTR + 1, CHUNK + CHUNKS:CHUNK + 2 * CHUNKS].bitcast(I32)
        hidden = sb("hidden", [P, UNROLL, TILES * D])
        space = sb("space", [P, UNROLL * ROWS * D])
        mask = space[:, 0:2 * TILES * WINDOW].rearrange("p (k t w) -> p k t w", k=2, t=TILES)
        mask_wide = space[:, 0:TILES * WIDE].rearrange("p (t w) -> p t w", t=TILES)
        h_early_t = space[:, 2 * CHUNK:3 * CHUNK]
        h_early = space[:, 3 * CHUNK:4 * CHUNK].rearrange("p (t d) -> p t d", t=TILES)
        dst_chunks = attr_space[0:CP, :].bitcast(I32).rearrange("p (k f) -> p k f", k=UNROLL)
        part_space = sb("part_space", [P, 3 * WINDOW])
        part = part_space[:, 0:2 * WINDOW].rearrange("p (k w) -> p k w", k=2)
        mask_sum = part_space[:, 2 * WINDOW:3 * WINDOW]
        part_wide = part_space[:, 0:WIDE]

        index_early = sb("index_early", [P, EARLY, TILES], I32)
        early = sb("early", [P, EARLY, TILES, D])
        stats_early = sb("stats_early", [P, TILES, 6])
        sum_early = sb("sum_early", [P, TILES])
        gap_early = sb("gap_early", [P, TILES])
        squares_early = sb("squares_early", [P, TILES])
        rstd_early = sb("rstd_early", [P, TILES])
        shift_early = sb("shift_early", [P, TILES])

        stats = part_space[0:NP, 0:BLOCK * 6].rearrange("p (b q) -> p b q", q=6)
        mean_sum = sb("mean_sum", [NP, BLOCK])
        mean_gap = sb("mean_gap", [NP, BLOCK])
        squares = sb("squares", [NP, BLOCK])
        rstd = sb("rstd", [NP, J])
        shift = sb("shift", [NP, J])
        table_out = space[0:NP, :].rearrange("p (k r d) -> p k r d", k=UNROLL, r=ROWS)
        iota_sb = space[:, 0:WIDE]
        h = rows[0:NP, :, 0:ROWS, :]
        h_t = hidden[:, :, 0:ROWS * NP]
        u = h_t

        pre = ps("pre", [P, 2, 1024])
        seg = ps("seg", [P, 2, 512])
        iota_ps = ps("iota_ps", [P, 512])
        spare = ps("spare", [P, 512])
        iota = iota_ps[:, 0:WIDE]
        bank = [pre[:, 0, 0:512], pre[:, 0, 512:1024], pre[:, 1, 0:512], pre[:, 1, 512:1024], iota_ps[:, :]]

        w_loaded = sem("w_loaded")
        w_late_loaded = sem("w_late_loaded")
        dst_loaded = sem("dst_loaded")
        cols_loaded = sem("cols_loaded")
        x_loaded = [sem(f"x_loaded{k}") for k in range(UNROLL)]
        x_block_loaded = [sem(f"x_block{b}_loaded") for b in range(1, 4)]
        consts_made = sem("consts_made")
        iota_made = sem("iota_made")
        iota_moved = sem("iota_moved")
        prod_ready = sem("prod_ready")
        b_rep_made = sem("b_rep_made")
        both_made = sem("both_made")
        dve_step = sem("dve_step")
        bounds_made = sem("bounds_made")
        ranges_stored = sem("ranges_stored")
        base_loaded = sem("base_loaded")
        span_known = sem("span_known")
        stats_taken = sem("stats_taken")
        stats_made = sem("stats_made")
        halves_joined = sem("halves_joined")
        rstd_made = sem("rstd_made")
        deviation_made = sem("deviation_made")
        scales_made = sem("scales_made")
        h_made = sem("h_made")
        h_turned = sem("h_turned")
        h_t_made = sem("h_t_made")
        table_ready = sem("table_ready")
        update_ready = sem("update_ready")
        table_made = sem("table_made")
        update_made = sem("update_made")
        table_stored = [sem(f"table_stored{k}") for k in range(UNROLL)]
        pool_turns = sem("pool_turns")
        act_turns = sem("act_turns")
        index_loaded = [sem(f"index_loaded{k}") for k in range(UNROLL)]
        attr_loaded = [sem(f"attr_loaded{k}") for k in range(UNROLL)]
        gathered = [sem(f"gathered{k}") for k in range(UNROLL)]
        pre_ready = sem("pre_ready")
        summed = sem("summed")
        relued = sem("relued")
        masks_made = sem("masks_made")
        mask_sums_made = sem("mask_sums_made")
        hidden_summed = sem("hidden_summed")
        part_copied = sem("part_copied")
        seg_ready = sem("seg_ready")
        accumulated = sem("accumulated")
        rel_made = sem("rel_made")
        wide_masks = sem("wide_masks")
        wide_ready = sem("wide_ready")
        wide_added = sem("wide_added")
        wide_copied = sem("wide_copied")
        wide_summed = sem("wide_summed")
        x_biased = sem("x_biased")
        edges_done = sem("edges_done")
        index_early_loaded = sem("index_early_loaded")
        gathered_early = sem("gathered_early")
        attr_early_loaded = sem("attr_early_loaded")
        early_stats = sem("early_stats")
        early_joined = sem("early_joined")
        early_squares = sem("early_squares")
        early_deviation = sem("early_deviation")
        early_rstd = sem("early_rstd")
        early_scales = sem("early_scales")
        early_normal = sem("early_normal")
        early_turned = sem("early_turned")
        early_moved = sem("early_moved")
        u_relued = sem("u_relued")
        o_ready = sem("o_ready")
        o_made = sem("o_made")
        out_stored = sem("out_stored")

        W_LOADS = [(w_src_sb[:, :], w_src), (w_node_sb[:, :], w_node), (b_msg1_bc[:, :], b_msg1.to_broadcast([P, D])),
                   (b_upd1_col[:, :], b_upd1)]
        W_LATE = [(w_msg2_t_sb[:, :], w_msg2_t), (b_msg2_col[:, :], b_msg2), (w_agg_sb[:, :], w_agg),
                  (w_attr_sb[0:K_ATTR, :], w_attr), (w_attr_sb[K_ATTR:, :], w_attr), (w_upd2_sb[:, :], w_upd2),
                  (b_upd2_bc[:, :], b_upd2.to_broadcast([P, D]))]

        block = ctx.enter_context(nc.Block())

        @block.sync
        def _(sp):
            sp.dma_start(index_early[:, :, :], src[0:EARLY].rearrange("c p t -> p c t")).then_inc(index_early_loaded, 16)
            for k in range(UNROLL):
                j = k * ROWS
                sp.dma_start(x_all[0:CUT[0][1], j:j + ROWS, :], x_rows[0:CUT[0][1], j:j + ROWS, :]).then_inc(x_loaded[k], 16)
            sp.wait_ge(w_loaded, 16 * len(W_LOADS))
            for b, loaded in enumerate(x_block_loaded, 1):
                j, end = b * BLOCK, J if b == 3 else (b + 1) * BLOCK
                for p, q in CUT:
                    sp.dma_start(x_all[p:q, j:end, :], x_rows[p:q, j:end, :]).then_inc(loaded, 16)
            for tile, source in W_LATE:
                sp.dma_start(tile, source).then_inc(w_late_loaded, 16)

            def load_index(i, k):
                sp.dma_start(index[:, k, :], src[bass.ds(i * UNROLL + (k + EARLY), 1)].rearrange("a p t -> p (a t)"))\
                    .then_inc(index_loaded[k], 16)

            for k in range(UNROLL):
                load_index(0, k)

            def store_table(i):
                for k in range(UNROLL):
                    g = i * UNROLL + k
                    sp.wait_ge(table_made, after(g))
                    for p, q in CUT:
                        sp.dma_start(table_rows[p:q, bass.ds(g * ROWS, ROWS), :], table_out[p:q, k])\
                            .then_inc(table_stored[k], 16)

            store_table(0)
            for p, q in CUT_DST:
                sp.dma_start(dst_chunks[p:q], dst_rows[p:q]).then_inc(dst_loaded, 16)
            store_table(1)
            sp.dma_start(dst_sb, dst_cols).then_inc(cols_loaded, 16)
            with sp.Fori(2, GBODIES) as i:
                store_table(i)

            sp.wait_ge(bounds_made, 2 * UNROLL + 1)
            sp.dma_start(ranges[0].rearrange("(p k) -> p k", k=UNROLL), bounds[:, 0, :]).then_inc(ranges_stored, 16)
            sp.dma_start(ranges[1].rearrange("(p k) -> p k", k=UNROLL), bounds[:, 2, :]).then_inc(ranges_stored, 16)
            sp.wait_ge(ranges_stored, 32)
            sp.dma_start(base_bc[:, :], ranges[0:1, :].to_broadcast([P, CHUNKS])).then_inc(base_loaded, 16)
            sp.dma_start(span_row, ranges[1:2, :]).then_inc(base_loaded, 16)

            def load_chunks(i, n, back, first=False):
                for k in range(UNROLL):
                    c = i * UNROLL + (k + EARLY)
                    sp.wait_ge(summed, after(n + k, back))
                    if not first:
                        load_index(i, k)
                    sp.dma_start(attrs[:, k, :], attr[bass.ds(c, 1)].rearrange("a f e -> f (a e)"))\
                        .then_inc(attr_loaded[k], 16)

            def load_pair(i, first=False):
                load_chunks(i * 2, i * PAIR, UNROLL, first)
                sp.wait_ge(summed, after(i * PAIR, UNROLL + 1))
                sp.dma_start(attrs_early, attr[bass.ds(i, 1)].rearrange("a f e -> f (a e)")).then_inc(attr_early_loaded, 16)
                load_chunks(i * 2 + 1, i * PAIR + (UNROLL + 1), UNROLL + 1)

            load_pair(0, first=True)
            with sp.Fori(1, EARLY) as i:
                load_pair(i)
            with sp.Fori(2 * EARLY, BODIES) as i:
                load_chunks(i, i * UNROLL + EARLY, UNROLL)

            def store(g, groups):
                sp.wait_ge(o_made, after(g + groups - 1))
                for p, q in CUT:
                    sp.dma_start(out_rows[p:q, bass.ds(g * ROWS, groups * ROWS), :],
                                 x_all[p:q, bass.ds(g * ROWS, groups * ROWS), :]).then_inc(out_stored, 16)

            with sp.Fori(0, GBODIES - 1) as i:
                store(i * UNROLL, UNROLL)
            LAST = [4, 1]
            for n, groups in enumerate(LAST):
                store(GROUPS - UNROLL + sum(LAST[:n]), groups)
            sp.wait_ge(out_stored, 16 * len(CUT) * (GBODIES - 1 + len(LAST)))

        @block.gpsimd
        def _(pool):
            pool.memset(identity[:, :], 1.0).then_inc(pool_turns, 1)
            pool.wait_ge(pool_turns, 1)
            pool.affine_select(out=identity[:, :], in_=identity[:, :], compare_op=ALU.is_equal, fill=0.0, base=0,
                               pattern=[[-1, P]], channel_multiplier=1).then_inc(consts_made, 1)
            pool.memset(eps[:, :], EPS).then_inc(consts_made, 1)
            pool.iota(iota_sb, pattern=[[1, WIDE]], base=0, channel_multiplier=0,
                      allow_small_or_imprecise_dtypes=True).then_inc(iota_made, 1)

            pool.wait_ge(index_early_loaded, 16)
            for c in range(EARLY):
                for t in range(TILES):
                    pool.indirect_dma_start(early[:, c, t, :], None, x, bass.IndirectOffsetOnAxis(index_early[:, c, t:t + 1], 0))\
                        .then_inc(gathered_early, 16)

            for k in range(UNROLL):
                pool.wait_ge(table_stored[k], 16 * len(CUT) * GBODIES)
            with pool.Fori(0, BODIES) as i:
                for k in range(UNROLL):
                    pool.wait_ge(index_loaded[k], i * 16 + 16)
                    pool.sem_inc(pool_turns, 1)
                    for t in range(TILES):
                        pool.indirect_dma_start(rows[:, k, t, :], None, table,
                                                bass.IndirectOffsetOnAxis(index[:, k, t:t + 1], 0))\
                            .then_inc(gathered[k], 16)

        @block.tensor
        def _(pe):
            pe.wait_ge(w_loaded, 16 * len(W_LOADS))
            pe.wait_ge(consts_made, 2)

            def turn_h(g, k):
                pe.wait_ge(h_made, after(g))
                pe.wait_ge(h_t_made, after(g, BACK[k]))
                for r in range(ROWS):
                    last = pe.transpose(pre[:, k % 2, r * NP:(r + 1) * NP], h[:, k, r, :], identity[0:NP, 0:NP])
                last.then_inc(h_turned, 1)

            def node_products(g, k):
                pe.wait_ge(h_t_made, after(g))
                pe.wait_ge(table_made, after(g, BACK[k]))
                for r in range(ROWS):
                    last = pe.matmul(seg[0:NP, k % 2, r * D:(r + 1) * D], h_t[:, k, r * NP:(r + 1) * NP],
                                     w_src_sb[:, :], start=True, stop=True)
                last.then_inc(table_ready, 1)
                pe.wait_ge(update_made, after(g, BACK[k]))
                pe.matmul(pre[:, k % 2, 512:512 + ROWS * NP], w_node_sb[:, :], h_t[:, k, :],
                          start=True, stop=True).then_inc(update_ready, 1)

            def node_groups(i, last):
                for k in range(UNROLL):
                    if not last or k + 1 < UNROLL:
                        turn_h(i * UNROLL + (k + 1), (k + 1) % UNROLL)
                    node_products(i * UNROLL + k, k)

            turn_h(0, 0)
            with pe.Fori(0, GBODIES - 1) as i:
                node_groups(i, False)
            node_groups(GBODIES - 1, True)

            pe.wait_ge(w_late_loaded, 16 * len(W_LATE))
            pe.wait_ge(b_rep_made, 1)
            pe.matmul(spare[:, 0:D], w_msg2_t_sb[:, :], w_agg_sb[:, :], start=True, stop=True)
            pe.matmul(spare[:, D:2 * D], b_msg2_rep[:, :], w_agg_sb[:, :], start=True, stop=True).then_inc(prod_ready, 1)

            def attr_products(i, n, k, back):
                pe.wait_ge(attr_loaded[k], i * 16 + 16)
                pe.wait_ge(summed, after(n + k, back[k]))
                for t in range(TILES):
                    last = pe.matmul(pre[:, k % 2, t * D:(t + 1) * D], attrs[:, k, t * P:(t + 1) * P],
                                     w_attr_sb[0:K_ATTR, :], start=True, stop=True)
                last.then_inc(pre_ready, 1)

            def early_products(i, n):
                pe.wait_ge(attr_early_loaded, i * 16 + 16)
                pe.wait_ge(early_moved, i + 1)
                pe.wait_ge(summed, after(n + UNROLL, 2))
                for t in range(TILES):
                    pe.matmul(pre[:, UNROLL % 2, t * D:(t + 1) * D], attrs_early[:, t * P:(t + 1) * P],
                              w_attr_sb[K_ATTR:, :], start=True, stop=False)
                    last = pe.matmul(pre[:, UNROLL % 2, t * D:(t + 1) * D], h_early_t[:, t * P:(t + 1) * P],
                                     w_src_sb[:, :], start=False, stop=True)
                last.then_inc(pre_ready, 1)

            def turn_early(i, n):
                pe.wait_ge(early_normal, i + 1)
                pe.wait_ge(summed, after(n + 3))
                for t in range(TILES):
                    last = pe.transpose(pre[:, 1, t * P:(t + 1) * P], h_early[:, t, :], identity[:, :])
                last.then_inc(early_turned, 1)

            def hidden_slot(k):
                return k if k < UNROLL else 2

            def hidden_sums(n, k):
                pe.wait_ge(masks_made, n + (k + 1))
                pe.wait_ge(relued, n + (k + 1))
                pe.wait_ge(part_copied, after(n + k, 1))
                for t in range(TILES):
                    last = pe.matmul(seg[:, 0, 0:WINDOW], hidden[:, hidden_slot(k), t * D:(t + 1) * D],
                                     mask[:, k % 2, t, :], start=(t == 0), stop=(t == TILES - 1))
                last.then_inc(hidden_summed, 1)

            def update_sums(n, k):
                pe.wait_ge(part_copied, after(n + k))
                pe.wait_ge(mask_sums_made, after(n + k))
                pe.wait_ge(accumulated, after(n + k, 1))
                pe.matmul(seg[:, 1, 0:WINDOW], w_both[:, :], part[:, k % 2, :], start=True, stop=False)
                pe.matmul(seg[:, 1, 0:WINDOW], bias_both[:, :], mask_sum, start=False, stop=True).then_inc(seg_ready, 1)

            def wide_sums(n, k):
                with pe.Fori(0, WINDOWS) as w:
                    pe.wait_ge(relued, n + (k + 1))
                    pe.wait_ge(wide_masks, (n + k) * WINDOWS + w + 1)
                    for t in range(TILES):
                        last = pe.matmul(seg[:, 0, 0:WIDE], hidden[:, hidden_slot(k), t * D:(t + 1) * D],
                                         mask_wide[:, t, :], start=(t == 0), stop=(t == TILES - 1))
                    last.then_inc(wide_summed, 1)
                    for t in range(TILES):
                        pe.matmul(seg[:, 1, 0:WIDE], bias_both[:, :], mask_wide[:, t, :], start=(t == 0), stop=False)
                    pe.wait_ge(wide_copied, (n + k) * WINDOWS + w + 1)
                    pe.matmul(seg[:, 1, 0:WIDE], w_both[:, :], part_wide, start=False, stop=True)\
                        .then_inc(wide_ready, 1)

            def edge_steps(i, n, wide, back=BACK, early=None):
                steps = UNROLL if early is None else UNROLL + 1
                for k in range(steps):
                    if k < UNROLL:
                        attr_products(i, n, k, back)
                    else:
                        early_products(early, n)
                    if early is not None and k == 4:
                        turn_early(early, n)
                    if wide:
                        wide_sums(n, k)
                    else:
                        if k >= 1:
                            hidden_sums(n, k - 1)
                        if k >= 2:
                            update_sums(n, k - 2)
                if not wide:
                    hidden_sums(n, steps - 1)
                    update_sums(n, steps - 2)
                    update_sums(n, steps - 1)

            def edge_loops(wide):
                with pe.Fori(0, EARLY) as i:
                    edge_steps(i * 2, i * PAIR, wide, early=i)
                    edge_steps(i * 2 + 1, i * PAIR + (UNROLL + 1), wide, BACK_AFTER_SIX)
                with pe.Fori(2 * EARLY, BODIES) as i:
                    edge_steps(i, i * UNROLL + EARLY, wide)

            pe.wait_ge(both_made, 2)
            pe.wait_ge(update_made, after(GROUPS - 1))
            pe.wait_ge(span_known, 1)
            span = pe.value_load(span_int[0:1, 0:1], min_val=0, max_val=N)
            with pe.If(span < WINDOW):
                edge_loops(wide=False)
            with pe.Else():
                edge_loops(wide=True)

            with pe.Fori(0, GBODIES) as i:
                for k in range(UNROLL):
                    g = i * UNROLL + k
                    pe.wait_ge(u_relued, after(g))
                    pe.wait_ge(o_made, after(g, UNROLL))
                    for r in range(ROWS):
                        last = pe.matmul(bank[k][0:NP, r * D:(r + 1) * D], u[:, k, r * NP:(r + 1) * NP], w_upd2_sb[:, :],
                                         start=True, stop=True)
                    last.then_inc(o_ready, 1)

        @block.scalar
        def _(act):
            for k in range(UNROLL):
                j = k * ROWS
                act.dma_start(x_all[CUT[1][0]:NP, j:j + ROWS, :], x_rows[CUT[1][0]:NP, j:j + ROWS, :]).then_inc(x_loaded[k], 16)
            for tile, source in W_LOADS:
                act.dma_start(tile, source).then_inc(w_loaded, 16)
            for credited in (h_made, u_relued, update_made, update_ready, h_turned, hidden_summed, seg_ready, o_ready):
                act.sem_inc(credited, CREDIT)
            act.wait_ge(consts_made, 2)
            act.activation(rstd_early[:, 0:1], eps[:, :], ACT.Sqrt)

            def deviation(i):
                act.wait_ge(stats_made, i + 1)
                act.sem_inc(act_turns, 1)
                j = i * BLOCK
                act.activation(rstd[:, bass.ds(j, BLOCK)], squares[:, :], ACT.Sqrt,
                               scale=1.0 / D, bias=eps[0:NP, :]).then_inc(deviation_made, 1)

            def normalise(g, k):
                act.wait_ge(h_turned, after(g, UNROLL))
                act.sem_inc(act_turns, 1)
                for r in range(ROWS):
                    j = g * ROWS + r
                    last = act.activation(h[:, k, r, :], x_all[:, bass.ds(j, 1), :].rearrange("p a d -> p (a d)"),
                                          ACT.Relu, scale=rstd[:, bass.ds(j, 1)], bias=shift[:, bass.ds(j, 1)])
                last.then_inc(h_made, 1)

            def update_out(g, k):
                act.wait_ge(update_ready, after(g))
                act.sem_inc(act_turns, 1)
                act.activation(update[:, 0:N].rearrange("f (p j) -> f j p", j=J)[:, bass.ds(g * ROWS, ROWS), :],
                               pre[:, k % 2, 512:512 + ROWS * NP].rearrange("f (r p) -> f r p", r=ROWS), ACT.Identity,
                               bias=b_upd1_col[:, :]).then_inc(update_made, 1)

            def node_groups(i, last):
                for k in range(UNROLL):
                    if not last or k + 2 < UNROLL:
                        if k + 2 == UNROLL:
                            act.wait_ge(scales_made, i + 2)
                            act.sem_inc(act_turns, 1)
                        normalise(i * UNROLL + (k + 2), (k + 2) % UNROLL)
                    if not last and k == 2:
                        deviation(i + 1)
                    update_out(i * UNROLL + k, k)

            deviation(0)
            act.wait_ge(scales_made, 1)
            normalise(0, 0)
            normalise(1, 1)
            act.wait_ge(w_loaded, 16 * len(W_LOADS))
            with act.Fori(0, GBODIES - 1) as i:
                node_groups(i, False)
            node_groups(GBODIES - 1, True)

            def relu_hidden(n, k):
                slot = k if k < UNROLL else 2
                act.wait_ge(summed, after(n + k))
                act.activation(hidden[:, slot, :], hidden[:, slot, :], ACT.Relu).then_inc(relued, 1)

            def early_h(i, k):
                if k == 2:
                    act.wait_ge(early_squares, i + 1)
                    act.activation(rstd_early[:, :], squares_early[:, :], ACT.Sqrt, scale=1.0 / D, bias=eps[:, :])\
                        .then_inc(early_deviation, 1)
                if k == 3:
                    act.wait_ge(early_scales, i + 1)
                    act.sem_inc(act_turns, 1)
                    for t in range(TILES):
                        last = act.activation(h_early[:, t, :], early[:, bass.ds(i, 1), t, :].rearrange("p a d -> p (a d)"),
                                              ACT.Relu, scale=rstd_early[:, t:t + 1], bias=shift_early[:, t:t + 1])
                    last.then_inc(early_normal, 1)

            with act.Fori(0, EARLY) as i:
                for k in range(UNROLL + 1):
                    relu_hidden(i * PAIR, k)
                    early_h(i, k)
                for k in range(UNROLL):
                    relu_hidden(i * PAIR + (UNROLL + 1), k)
            with act.Fori(2 * EARLY, BODIES) as i:
                for k in range(UNROLL):
                    relu_hidden(i * UNROLL + EARLY, k)

            act.wait_ge(edges_done, 1)
            act.sem_inc(act_turns, 1)
            with act.Fori(0, GBODIES) as i:
                for k in range(UNROLL):
                    g = i * UNROLL + k
                    act.wait_ge(o_ready, after(g, UNROLL))
                    act.sem_inc(act_turns, 1)
                    act.activation(u[:, k].rearrange("f (r p) -> f r p", r=ROWS),
                                   update[:, 0:N].rearrange("f (p j) -> f j p", j=J)[:, bass.ds(g * ROWS, ROWS), :],
                                   ACT.Relu).then_inc(u_relued, 1)

        @block.vector
        def _(dve):
            for credited in (summed, mask_sums_made, part_copied, accumulated, h_t_made, table_made, o_made):
                dve.sem_inc(credited, CREDIT)

            dve.wait_ge(iota_made, 1)
            dve.tensor_copy(iota, iota_sb).then_inc(iota_moved, 1)

            dve.memset(update[:, N:PADDED], 0.0)

            def bound(piece):
                row, k = divmod(piece, UNROLL)
                dve.tensor_reduce(bounds[:, row, k:k + 1], dst_chunks[:, k, :], AX_X, (ALU.min, ALU.max)[row])\
                    .then_inc(bounds_made, 1)

            def join_bounds():
                dve.wait_ge(bounds_made, 2 * UNROLL)
                dve.tensor_tensor(bounds[:, 2, :], bounds[:, 1, :], bounds[:, 0, :], ALU.subtract).then_inc(bounds_made, 1)

            def statistics(i, k):
                for r in range(ROWS):
                    j = (i * UNROLL + k) * ROWS + r
                    last = dve.bn_stats(stats[:, k * ROWS + r, :],
                                        x_all[:, bass.ds(j, 1), :].rearrange("p a d -> p (a d)"))
                last.then_inc(stats_taken, 1)

            def join_statistics(i):
                dve.wait_ge(stats_taken, i * UNROLL + UNROLL)
                _, mean_e, squares_e, _, mean_o, squares_o = (stats[:, :, q] for q in range(6))
                dve.tensor_tensor(mean_sum[:, :], mean_e, mean_o, ALU.add).then_inc(halves_joined, 1)
                dve.tensor_tensor(mean_gap[:, :], mean_e, mean_o, ALU.subtract).then_inc(halves_joined, 1)
                dve.tensor_tensor(squares[:, :], squares_e, squares_o, ALU.add).then_inc(halves_joined, 1)
                dve.wait_ge(halves_joined, i * 4 + 3)
                dve.tensor_tensor(mean_gap[:, :], mean_gap[:, :], mean_gap[:, :], ALU.mult).then_inc(halves_joined, 1)
                dve.wait_ge(halves_joined, i * 4 + 4)
                dve.scalar_tensor_tensor(squares[:, :], mean_gap[:, :], D / 4.0, squares[:, :], ALU.mult, ALU.add)\
                    .then_inc(stats_made, 1)

            def scales(i):
                dve.wait_ge(deviation_made, i + 1)
                block = rstd[:, bass.ds(i * BLOCK, BLOCK)]
                dve.reciprocal(block, block).then_inc(rstd_made, 1)
                dve.wait_ge(rstd_made, i + 1)
                dve.scalar_tensor_tensor(shift[:, bass.ds(i * BLOCK, BLOCK)], mean_sum[:, :], -0.5, block,
                                         ALU.mult, ALU.mult).then_inc(scales_made, 1)

            def h_t_out(g, k):
                dve.wait_ge(h_turned, after(g))
                dve.wait_ge(update_ready, after(g, UNROLL))
                dve.tensor_copy(h_t[:, k, :], pre[:, k % 2, 0:ROWS * NP]).then_inc(h_t_made, 1)

            def table_rows_out(i, k, first):
                if not first:
                    dve.wait_ge(table_stored[k], i * (16 * len(CUT)))
                dve.wait_ge(table_ready, i * UNROLL + (k + 1))
                dve.tensor_tensor(table_out[:, k], seg[0:NP, k % 2, :].rearrange("p (r d) -> p r d", r=ROWS),
                                  b_msg1_bc[0:NP, :].unsqueeze(1).to_broadcast([NP, ROWS, D]), ALU.add)\
                    .then_inc(table_made, 1)

            def node_groups(i, more, first=False, pieces=()):
                between = {0: (1, 3), 1: (1, 4), 2: (2, 0), 3: (2, 1), 4: (2, 2)}
                for k in range(UNROLL):
                    if more > 0 or k + 1 < UNROLL:
                        h_t_out(i * UNROLL + (k + 1), (k + 1) % UNROLL)
                    ahead, group = between[k]
                    if more >= ahead:
                        if first and k == 2:
                            dve.wait_ge(x_block_loaded[1], 16 * len(CUT))
                        statistics(i + ahead, group)
                        if k == 1:
                            join_statistics(i + 1)
                    for piece in pieces[k] if pieces else ():
                        bound(piece)
                    table_rows_out(i, k, first)
                    if more > 0 and k == 2:
                        scales(i + 1)

            for k in range(UNROLL):
                dve.wait_ge(x_loaded[k], 16 * len(CUT))
                statistics(0, k)
            join_statistics(0)
            scales(0)
            h_t_out(0, 0)
            dve.wait_ge(x_block_loaded[0], 16 * len(CUT))
            for k in range(3):
                statistics(1, k)
            dve.wait_ge(w_loaded, 16 * len(W_LOADS))
            node_groups(0, 2, first=True)
            dve.wait_ge(x_block_loaded[2], 16 * len(CUT))
            with dve.Fori(1, GBODIES - 2) as i:
                node_groups(i, 2)
            dve.wait_ge(dst_loaded, 16 * len(CUT_DST))
            node_groups(GBODIES - 2, 1, pieces=[[], [], [0], [1], [2]])
            node_groups(GBODIES - 1, 0, pieces=[[3, 4], [5, 6], [7, 8], [9], []])
            join_bounds()

            dve.wait_ge(w_late_loaded, 16 * len(W_LATE))
            dve.tensor_copy(b_msg2_rep[:, :], b_msg2_col[:, 0:1].to_broadcast([D, P])).then_inc(b_rep_made, 1)
            dve.wait_ge(base_loaded, 32)
            dve.tensor_copy(base_row, base_bc[K_ATTR:K_ATTR + 1, :]).then_inc(dve_step, 1)
            dve.tensor_reduce(span_max[:, :], span_row, AX_X, ALU.max).then_inc(dve_step, 1)
            dve.wait_ge(dve_step, 2)
            dve.tensor_copy(span_int[:, :], span_max[:, :]).then_inc(span_known, 1)
            dve.wait_ge(cols_loaded, 16)
            dve.tensor_tensor(dst_rel[:, :, :], dst_sb,
                              base_bc[:, :].unsqueeze(2).to_broadcast([P, CHUNKS, TILES]), ALU.subtract)\
                .then_inc(dve_step, 1)

            def sum_rows(i, n, k):
                dve.wait_ge(pre_ready, n + (k + 1))
                if k < UNROLL:
                    dve.wait_ge(gathered[k], i * (16 * TILES) + 16 * TILES)
                    dve.tensor_tensor(hidden[:, k, :], pre[:, k % 2, 0:TILES * D],
                                      rows[:, k].rearrange("p t d -> p (t d)"), ALU.add).then_inc(summed, 1)
                else:
                    dve.tensor_tensor(hidden[:, 2, :].rearrange("p (t d) -> p t d", t=TILES),
                                      pre[:, k % 2, 0:TILES * D].rearrange("p (t d) -> p t d", t=TILES),
                                      b_msg1_bc[:, :].unsqueeze(1).to_broadcast([P, TILES, D]), ALU.add)\
                        .then_inc(summed, 1)

            def early_rows(i, k):
                if k == 0:
                    for t in range(TILES):
                        last = dve.bn_stats(stats_early[:, t, :], early[:, bass.ds(i, 1), t, :].rearrange("p a d -> p (a d)"))
                    last.then_inc(early_stats, 1)
                if k == 1:
                    dve.wait_ge(early_stats, i + 1)
                    _, mean_e, squares_e, _, mean_o, squares_o = (stats_early[:, :, q] for q in range(6))
                    dve.tensor_tensor(sum_early[:, :], mean_e, mean_o, ALU.add).then_inc(early_joined, 1)
                    dve.tensor_tensor(gap_early[:, :], mean_e, mean_o, ALU.subtract).then_inc(early_joined, 1)
                    dve.tensor_tensor(squares_early[:, :], squares_e, squares_o, ALU.add).then_inc(early_joined, 1)
                    dve.wait_ge(early_joined, i * 4 + 3)
                    dve.tensor_tensor(gap_early[:, :], gap_early[:, :], gap_early[:, :], ALU.mult).then_inc(early_joined, 1)
                    dve.wait_ge(early_joined, i * 4 + 4)
                    dve.scalar_tensor_tensor(squares_early[:, :], gap_early[:, :], D / 4.0, squares_early[:, :],
                                             ALU.mult, ALU.add).then_inc(early_squares, 1)
                if k == 2:
                    dve.wait_ge(early_deviation, i + 1)
                    dve.reciprocal(rstd_early[:, :], rstd_early[:, :]).then_inc(early_rstd, 1)
                    dve.wait_ge(early_rstd, i + 1)
                    dve.scalar_tensor_tensor(shift_early[:, :], sum_early[:, :], -0.5, rstd_early[:, :],
                                             ALU.mult, ALU.mult).then_inc(early_scales, 1)
                if k == 4:
                    dve.wait_ge(early_turned, i + 1)
                    dve.tensor_copy(h_early_t, pre[:, 1, 0:TILES * P]).then_inc(early_moved, 1)

            def make_masks(c, n, k, back):
                dve.wait_ge(hidden_summed, after(n + k, back[k]))
                dve.wait_ge(mask_sums_made, after(n + k, back[k]))
                dve.tensor_tensor(mask[:, k % 2], iota[:, 0:WINDOW].unsqueeze(1).to_broadcast([P, TILES, WINDOW]),
                                  dst_rel[:, bass.ds(c, 1), :].rearrange("p a t -> p (a t)").unsqueeze(2)
                                  .to_broadcast([P, TILES, WINDOW]), ALU.is_equal).then_inc(masks_made, 1)

            def sum_masks(n, k):
                dve.wait_ge(masks_made, n + (k + 1))
                dve.wait_ge(seg_ready, after(n + k, 1))
                dve.tensor_reduce(mask_sum, mask[:, k % 2].rearrange("p t w -> p w t"), AX_X, ALU.add)\
                    .then_inc(mask_sums_made, 1)

            def copy_sums(n, k, back):
                dve.wait_ge(hidden_summed, after(n + k))
                dve.wait_ge(seg_ready, after(n + k, back[k]))
                dve.tensor_copy(part[:, k % 2, :], seg[:, 0, 0:WINDOW]).then_inc(part_copied, 1)

            def accumulate(c, n, k):
                base = dve.value_load(base_row[0:1, bass.ds(c, 1)], min_val=0, max_val=N - 1)
                dve.wait_ge(seg_ready, after(n + k))
                dve.wait_ge(accumulated, after(n + k, 1))
                columns = update[:, bass.ds(base, WINDOW)]
                dve.tensor_tensor(columns, seg[:, 1, 0:WINDOW], columns, ALU.add).then_inc(accumulated, 1)

            def accumulate_wide(c, n, k):
                dve.tensor_scalar(rel[:, :], dst_rel[:, bass.ds(c, 1), :].rearrange("p a t -> p (a t)"),
                                  base_bc[:, bass.ds(c, 1)], None, ALU.add).then_inc(rel_made, 1)
                with dve.Fori(0, WINDOWS) as w:
                    m = (n + k) * WINDOWS + w
                    dve.wait_ge(rel_made, m + n + (k + 1))
                    dve.tensor_tensor(mask_wide, iota.unsqueeze(1).to_broadcast([P, TILES, WIDE]),
                                      rel[:, :].unsqueeze(2).to_broadcast([P, TILES, WIDE]), ALU.is_equal)\
                        .then_inc(wide_masks, 1)
                    dve.wait_ge(wide_masks, m + 1)
                    dve.tensor_scalar(rel[:, :], rel[:, :], -float(WIDE), None, ALU.add).then_inc(rel_made, 1)
                    dve.wait_ge(wide_summed, m + 1)
                    dve.tensor_copy(part_wide, seg[:, 0, 0:WIDE]).then_inc(wide_copied, 1)
                    dve.wait_ge(wide_ready, m + 1)
                    columns = update[:, bass.ds(w * WIDE, WIDE)]
                    dve.tensor_tensor(columns, seg[:, 1, 0:WIDE], columns, ALU.add).then_inc(wide_added, 1)
                    dve.wait_ge(wide_added, m + 1)

            def edge_steps(i, n, wide, back=BACK, early=None):
                steps = UNROLL if early is None else UNROLL + 1

                def chunk(k):
                    return i * UNROLL + (k + EARLY) if k < UNROLL else early

                for k in range(steps):
                    if not wide:
                        make_masks(chunk(k), n, k, back)
                    sum_rows(i, n, k)
                    if early is not None:
                        early_rows(early, k)
                    if wide:
                        accumulate_wide(chunk(k), n, k)
                    else:
                        if k >= 1:
                            copy_sums(n, k - 1, back)
                        if k >= 2:
                            accumulate(chunk(k - 2), n, k - 2)
                        if k >= 1:
                            sum_masks(n, k - 1)
                if not wide:
                    copy_sums(n, steps - 1, back)
                    accumulate(chunk(steps - 2), n, steps - 2)
                    sum_masks(n, steps - 1)
                    accumulate(chunk(steps - 1), n, steps - 1)

            def edge_loops(wide):
                with dve.Fori(0, EARLY) as i:
                    edge_steps(i * 2, i * PAIR, wide, early=i)
                    edge_steps(i * 2 + 1, i * PAIR + (UNROLL + 1), wide, BACK_AFTER_SIX)
                with dve.Fori(2 * EARLY, 2 * EARLY + GROUPS) as i:
                    rows_g = x_all[:, bass.ds((i - 2 * EARLY) * ROWS, ROWS), :]
                    dve.tensor_tensor(rows_g, rows_g, b_upd2_bc[0:NP, :].unsqueeze(1).to_broadcast([NP, ROWS, D]), ALU.add)\
                        .then_inc(x_biased, 1)
                    edge_steps(i, i * UNROLL + EARLY, wide)
                with dve.Fori(2 * EARLY + GROUPS, BODIES) as i:
                    edge_steps(i, i * UNROLL + EARLY, wide)

            dve.wait_ge(h_made, after(GROUPS - 1))
            dve.wait_ge(prod_ready, 1)
            dve.tensor_copy(w_both[:, :], spare[:, 0:D]).then_inc(both_made, 1)
            dve.tensor_copy(bias_both[:, :], spare[:, D:2 * D]).then_inc(both_made, 1)
            dve.wait_ge(update_made, after(GROUPS - 1))
            dve.wait_ge(span_known, 1)
            dve.wait_ge(iota_moved, 1)
            dve.wait_ge(dve_step, 3)
            for k in range(UNROLL):
                dve.wait_ge(table_stored[k], 16 * len(CUT) * GBODIES)
            dve.wait_ge(gathered_early, 16 * EARLY * TILES)
            span = dve.value_load(span_int[0:1, 0:1], min_val=0, max_val=N)
            with dve.If(span < WINDOW):
                edge_loops(wide=False)
            with dve.Else():
                edge_loops(wide=True)
            dve.drain().then_inc(edges_done, 1)

            dve.wait_ge(x_biased, GROUPS)
            with dve.Fori(0, GBODIES) as i:
                for k in range(UNROLL):
                    g = i * UNROLL + k
                    rows_g = x_all[:, bass.ds(g * ROWS, ROWS), :]
                    dve.wait_ge(o_ready, after(g))
                    dve.tensor_tensor(rows_g, bank[k][0:NP, :].rearrange("p (r d) -> p r d", r=ROWS), rows_g, ALU.add)\
                        .then_inc(o_made, 1)


def kernel(x, src, dst, edge_attr_64, L0_gnn_msg_w1, L0_gnn_msg_b1, L0_gnn_msg_w2, L0_gnn_msg_b2, L0_gnn_upd_w1,
           L0_gnn_upd_b1, L0_gnn_upd_w2, L0_gnn_upd_b2):
    import numpy as np
    import concourse.bacc as bacc
    from concourse.bass_utils import run_bass_kernel_spmd

    x, src, dst, attr = (np.asarray(a) for a in (x, src, dst, edge_attr_64))
    w1, b1, w2, b2 = (np.asarray(a) for a in (L0_gnn_msg_w1, L0_gnn_msg_b1, L0_gnn_msg_w2, L0_gnn_msg_b2))
    u1, ub1, u2, ub2 = (np.asarray(a) for a in (L0_gnn_upd_w1, L0_gnn_upd_b1, L0_gnn_upd_w2, L0_gnn_upd_b2))
    n, d = x.shape
    e, k_attr = attr.shape
    chunks = e // CHUNK
    arrays = {
        "x": x,
        "src": src.reshape(chunks, TILES, P).transpose(0, 2, 1),
        "dst_rows": dst.reshape(chunks // UNROLL, UNROLL, CHUNK),
        "dst_cols": dst.reshape(chunks, TILES, P).transpose(2, 0, 1),
        "attr": attr.reshape(chunks, CHUNK, k_attr).transpose(0, 2, 1),
        "w_src": w1[:d], "w_attr": w1[d:], "b_msg1": b1.reshape(1, d), "w_msg2_t": w2.T, "b_msg2": b2.reshape(d, 1),
        "w_node": u1[:d], "w_agg": u1[d:], "b_upd1": ub1.reshape(d, 1), "w_upd2": u2, "b_upd2": ub2.reshape(1, d),
    }
    nc = bacc.Bacc("TRN2", target_bir_lowering=False, num_devices=1)
    arrays = {"in_" + name: np.ascontiguousarray(a) for name, a in arrays.items()}
    args = {name[3:]: nc.dram_tensor(name, a.shape, mybir.dt.from_np(a.dtype), kind="ExternalInput").ap()
            for name, a in arrays.items()}
    out = nc.dram_tensor("out", (n, d), F32, kind="ExternalOutput").ap()
    gnn_layer(nc, out=out, **args)
    return run_bass_kernel_spmd(nc, [arrays], core_ids=[0]).results[0]["out"]
```
